# Optimizing a Trainium2 kernel written in Bass

```python
import numpy as np
import jax
import jax.numpy as jnp

def _softmax(x, axis=-1):
    return jax.nn.softmax(x, axis=axis)

def _gelu(x):
    return jax.nn.gelu(x, approximate=True)

def _silu(x):
    return jax.nn.silu(x)

def _sigmoid(x):
    return jax.nn.sigmoid(x)

def _layernorm(x, axis=-1, eps=1e-05):
    m = jnp.mean(x, axis=axis, keepdims=True)
    v = jnp.var(x, axis=axis, keepdims=True)
    return (x - m) / jnp.sqrt(v + eps)

def _scatter_add(tgt, idx, src, axis=0):
    return tgt.at[idx].add(src)

def _segment_sum(src, seg, n):
    return jax.ops.segment_sum(src, seg, n)
kernel_name = 'mk_flamingo_gated_d1_seqx_r4_393fa5'

def setup_inputs(seed: int=0):
    np.random.seed(seed)
    _w = jnp.asarray

    def _rec_inputs():
        import jax
        import jax.numpy as jnp
        _rk = jax.random.key(seed)
        x = -0.0002928 + 1 * jax.random.normal(jax.random.fold_in(_rk, 1), (32, 128, 256), jnp.float32)
        _lenS = 128 - jax.random.randint(jax.random.fold_in(_rk, 7), (32,), 0, max(1, 128 // 4) + 1, jnp.int32)
        _lenS2 = 128 - jax.random.randint(jax.random.fold_in(_rk, 8), (32,), 0, max(1, 128 // 4) + 1, jnp.int32)
        _ctx_1024P = jax.random.normal(jax.random.fold_in(_rk, 11), (32, 16, 256), jnp.float32)
        _ctx_1024c = jax.random.dirichlet(jax.random.fold_in(_rk, 511), 0.3 * jnp.ones((16,), jnp.float32), (32, 128))
        _ctx_1024t = jnp.einsum('bsk,bkd->bsd', _ctx_1024c, _ctx_1024P)
        _ctx_1024t = _ctx_1024t * jax.lax.rsqrt(jnp.mean(jnp.square(_ctx_1024t)) + 1e-12) * 0.953939
        ctx_1024 = -1.39393e-06 + 0.999914 * (_ctx_1024t + 0.3 * jax.random.normal(jax.random.fold_in(_rk, 611), (32, 128, 256), jnp.float32))
        _validS = jnp.arange(128)[None, :] < _lenS[:, None]
        _validS2 = jnp.arange(128)[None, :] < _lenS2[:, None]
        _causal = jnp.tril(jnp.ones((128, 128), dtype=bool))
        mask_1x1xSxS2_bf1 = jnp.ones((1, 1, 128, 128), dtype=bool)
        _g = jax.random.normal(jax.random.fold_in(_rk, 9001), (2, 1), jnp.float32)
        _g = jnp.sign(_g) * jnp.maximum(jnp.abs(_g), 1.0) + (_g == 0) * 1.0
        g_xattn = _g[0]
        g_ffn = _g[1]
        return (x, ctx_1024, mask_1x1xSxS2_bf1, g_xattn, g_ffn)
    x, ctx_1024, mask_1x1xSxS2_bf1, g_xattn, g_ffn = _rec_inputs()

    def _L0_xattn_setup():
        import jax, jax.numpy as jnp
        import numpy as np
        H = 16
        HID = 64

        def _gelu(x):
            return jax.nn.gelu(x, approximate=False)
        key = jax.random.key(seed)
        ks = jax.random.split(key, 12)
        B, N, D = (2, 512, 256)
        Dh = D // H
        inp = {'query': jax.random.normal(ks[0], (B, N, D), jnp.float32), 'key': jax.random.normal(ks[1], (B, N, D), jnp.float32), 'value': jax.random.normal(ks[2], (B, N, D), jnp.float32), 'allowed_mask': jnp.ones((1, 1, N, N), dtype=bool), 'wq': jax.random.normal(ks[3], (D, D), jnp.float32) * D ** (-0.5), 'wk': jax.random.normal(ks[4], (D, D), jnp.float32) * D ** (-0.5), 'wv': jax.random.normal(ks[5], (D, D), jnp.float32) * D ** (-0.5), 'wo': jax.random.normal(ks[6], (D, D), jnp.float32) * D ** (-0.5), 'wb1': jax.random.normal(ks[7], (HID, 1), jnp.float32), 'wb2': jax.random.normal(ks[8], (H * Dh, HID), jnp.float32) * HID ** (-0.5), 'wg1': jax.random.normal(ks[9], (HID, Dh), jnp.float32) * Dh ** (-0.5), 'wg2': jax.random.normal(ks[10], (Dh, HID), jnp.float32) * HID ** (-0.5), 'n_context': 512}
        return inp
    _L0_xattn_all = _L0_xattn_setup()
    _L0_xattn_in = {k: v for k, v in _L0_xattn_all.items() if k in ('wq', 'wk', 'wv', 'wo', 'wb1', 'wb2', 'wg1', 'wg2')}
    del _L0_xattn_all

    def _L0_ffn_setup():
        import jax, jax.numpy as jnp
        import numpy as np
        EPS = 1e-09
        key = jax.random.key(seed)
        k0, k1, k2, k3 = jax.random.split(key, 4)
        B, S, H, F, E = (4, 512, 256, 512, 8)
        return {'hidden_states': jax.random.normal(k0, (B, S, H), dtype=jnp.float32), 'router_w': jax.random.normal(k1, (H, E), dtype=jnp.float32) * 0.02, 'w1': jax.random.normal(k2, (E, H, F), dtype=jnp.float32) * 0.02, 'w2': jax.random.normal(k3, (E, F, H), dtype=jnp.float32) * 0.02}
    _L0_ffn_all = _L0_ffn_setup()
    _L0_ffn_in = {k: v for k, v in _L0_ffn_all.items() if k in ('router_w', 'w1', 'w2')}
    del _L0_ffn_all
    return {'x': x, 'ctx_1024': ctx_1024, 'mask_1x1xSxS2_bf1': mask_1x1xSxS2_bf1, 'g_xattn': g_xattn, 'g_ffn': g_ffn, 'L0_xattn_wq': _L0_xattn_in['wq'], 'L0_xattn_wk': _L0_xattn_in['wk'], 'L0_xattn_wv': _L0_xattn_in['wv'], 'L0_xattn_wo': _L0_xattn_in['wo'], 'L0_xattn_wb1': _L0_xattn_in['wb1'], 'L0_xattn_wb2': _L0_xattn_in['wb2'], 'L0_xattn_wg1': _L0_xattn_in['wg1'], 'L0_xattn_wg2': _L0_xattn_in['wg2'], 'L0_ffn_router_w': _L0_ffn_in['router_w'], 'L0_ffn_w1': _L0_ffn_in['w1'], 'L0_ffn_w2': _L0_ffn_in['w2']}

def reference(x, ctx_1024, mask_1x1xSxS2_bf1, g_xattn, g_ffn, L0_xattn_wq, L0_xattn_wk, L0_xattn_wv, L0_xattn_wo, L0_xattn_wb1, L0_xattn_wb2, L0_xattn_wg1, L0_xattn_wg2, L0_ffn_router_w, L0_ffn_w1, L0_ffn_w2):
    import jax
    import jax.numpy as jnp

    def _L0_xattn_ref(query, key, value, allowed_mask, wq, wk, wv, wo, wb1, wb2, wg1, wg2, n_context):
        import jax, jax.numpy as jnp
        import numpy as np
        H = 16
        HID = 64

        def _gelu(x):
            return jax.nn.gelu(x, approximate=False)
        B, N, D = query.shape
        Dh = D // H

        def split_heads(x):
            return x.reshape(B, N, H, Dh).transpose(0, 2, 1, 3)
        q = split_heads(query @ wq.T)
        k = split_heads(key @ wk.T)
        v = split_heads(value @ wv.T)
        log_n = jnp.log(jnp.asarray(n_context, jnp.float32))
        base = (_gelu(log_n * wb1[:, 0]) @ wb2.T).reshape(1, H, 1, Dh)
        gate = 1.0 + jnp.tanh(_gelu(q @ wg1.T) @ wg2.T)
        q = q * base * gate
        scores = jnp.einsum('bhnd,bhmd->bhnm', q, k) / jnp.sqrt(jnp.float32(Dh))
        scores = jnp.where(allowed_mask, scores, -jnp.inf)
        attn = jax.nn.softmax(scores, axis=-1)
        out = jnp.einsum('bhnm,bhmd->bhnd', attn, v)
        out = out.transpose(0, 2, 1, 3).reshape(B, N, D)
        return out @ wo.T

    def _L0_ffn_ref(hidden_states, router_w, w1, w2):
        import jax, jax.numpy as jnp
        import numpy as np
        EPS = 1e-09
        TOP_K = 2
        orig_shape = hidden_states.shape
        H = orig_shape[-1]
        E = router_w.shape[-1]
        flat = hidden_states.reshape(-1, H)
        T = flat.shape[0]
        gate_logits = flat @ router_w
        gate_probs = jax.nn.softmax(gate_logits, axis=-1)
        topk_w, topk_idx = jax.lax.top_k(gate_probs, TOP_K)
        topk_w = topk_w / jnp.clip(topk_w.sum(-1, keepdims=True), EPS)
        cw = jnp.zeros((T, E), dtype=flat.dtype).at[jnp.arange(T)[:, None], topk_idx].add(topk_w)
        h = jax.nn.silu(jnp.einsum('td,edf->etf', flat, w1))
        y = jnp.einsum('etf,efd->etd', h, w2)
        out = jnp.einsum('etd,te->td', y, cw)
        return out.reshape(orig_shape)
    x = x + jnp.tanh(g_xattn[0]) * _L0_xattn_ref(_layernorm(x, axis=-1), ctx_1024, ctx_1024, mask_1x1xSxS2_bf1, L0_xattn_wq, L0_xattn_wk, L0_xattn_wv, L0_xattn_wo, L0_xattn_wb1, L0_xattn_wb2, L0_xattn_wg1, L0_xattn_wg2, 512)
    x = x + jnp.tanh(g_ffn[0]) * _L0_ffn_ref(_layernorm(x, axis=-1), L0_ffn_router_w, L0_ffn_w1, L0_ffn_w2)
    return x

_drawn_inputs = setup_inputs


def setup_inputs(seed=0):
    import zlib

    import numpy as np

    out = dict(_drawn_inputs(seed))
    spreads = {}
    factors = {}
    for name, (base, spread) in spreads.items():
        noise = np.random.default_rng([zlib.crc32(name.encode()), seed]).standard_normal(out[name].shape)
        drawn = base * np.exp(spread * noise) if base else spread * noise
        out[name] = jnp.asarray(drawn.astype(out[name].dtype))
    for name, factor in factors.items():
        out[name] = (out[name] * factor).astype(out[name].dtype)
    return out
```

```python
import math

import concourse.bass as bass
from concourse import mybir
from concourse.alu_op_type import AluOpType as ALU

F32 = mybir.dt.float32
BF16 = mybir.dt.bfloat16
U32 = mybir.dt.uint32
U8 = mybir.dt.uint8
ACT = mybir.ActivationFunctionType
AX = mybir.AxisListType

B, S, D = 32, 128, 256
H, DH = 16, 16
P = 128
T = 4
G = B // T
GT = T * S
KC = D // P
HC = H // KC
HID = 64
PAIRS = HC // 2
QH = 4
NQ = H // QH
TERMS_Q = (0, 0, 1, 0, 2, 1)
TERMS_K = (0, 1, 0, 2, 0, 1)
NT = len(TERMS_Q)
KR = NT * DH
MR = 3
VW = 32
TWO_ONES = 1.0 + 0x3f80 * 2.0 ** -23
NEG = -float(2.0 ** 100)
N_CONTEXT = 512
E, F = 8, 512
FC = F // P
TOK = B * S
REGION = TOK + P
TILES = 72
SPARE = TILES - 2 * TOK // P
PW = D + 4
PAD_ROWS = E * REGION
A_USES = 20
EPS = 1e-5
SMALL = 9
CONST_POOL = 18
LINKS = 107


def build(nc, x, ctxT, mask, maskT, gx, gf, wqT, wkT, wvT, woT, wb1, wb2T, gate1, gate2, wr, w1, w2, out):
    from contextlib import ExitStack

    x_t = x.rearrange("b s d -> s b d")
    ctx_t = ctxT.rearrange("(c p) t -> p c t", p=P)
    out_t = out.rearrange("b s d -> s b d")

    ctx = ExitStack()
    with ctx:
        def sb(name, shape, dt=F32):
            return ctx.enter_context(nc.sbuf_tensor(name, shape, dt))

        def sem(name):
            return ctx.enter_context(nc.semaphore(name))

        kparts_d = nc.dram_tensor("kparts_d", [D, 3, GT], BF16, kind="Internal").ap()
        qparts_d = nc.dram_tensor("qparts_d", [D, 3, GT], BF16, kind="Internal").ap()
        rows_d = nc.dram_tensor("rows_d", [E * REGION + SPARE * P, PW], F32, kind="Internal").ap()
        ffn_d = nc.dram_tensor("ffn_d", [2 * REGION, D], F32, kind="Internal").ap()

        xy = sb("xy", [P, B, D])
        stack = sb("stack", [P, 2, 2, H, GT], BF16)
        w1_sb = stack[:, 0, :, :, :].rearrange("p a h t -> p (a h t)").bitcast(F32)\
            .rearrange("p (e c f) -> p e c f", e=E, c=KC)
        w2_sb = stack[:, 1, :, :, :].rearrange("p a h t -> p (a h t)").bitcast(F32)\
            .rearrange("p (e c f) -> p e c f", e=E, c=FC)
        ident = sb("ident", [P, P])
        identb = sb("identb", [P, P], BF16)
        ones_b = sb("ones_b", [P, P], BF16)
        before = sb("before", [P, P], BF16)
        mask_u = sb("mask_u", [P, 2, P], U8)
        bias_b = sb("bias_b", [P, 2, P], BF16)
        seen = sb("seen", [P, 4])
        gates = sb("gates", [P, 2])
        graw = sb("graw", [P, 2])
        wq_sb, wk_sb, wv_sb, wo_sb = (sb(n, [P, KC, D]) for n in ("wq_sb", "wk_sb", "wv_sb", "wo_sb"))
        g1_sb = sb("g1_sb", [P, PAIRS, P])
        g2_sb = sb("g2_sb", [P, 2 * DH])
        wr_sb = sb("wr_sb", [P, KC, E])
        wb1_sb = sb("wb1_sb", [HID, 1])
        wb1g = sb("wb1g", [HID, 1])
        wb2_sb = sb("wb2_sb", [HID, D])
        base = sb("base", [P, KC])
        ctxg = sb("ctxg", [P, KC, GT])
        xn = sb("xn", [P, T, D])
        xnT = sb("xnT", [P, KC, GT])
        qT = sb("qT", [P, KC, GT])
        kT = sb("kT", [P, KC, GT])
        th = sb("th", [P, KC, GT])
        hid = sb("hid", [P, PAIRS, GT])
        rest = sb("rest", [P, GT])
        krest = sb("krest", [P, GT])
        q3 = sb("q3", [P, KC, 3, GT], BF16)
        k3 = sb("k3", [P, KC, 3, GT], BF16)
        v = sb("v", [P, T, H, VW])
        pT = sb("pT", [P, NQ, QH * P])
        stats = sb("stats", [P, T, 6])
        mv = sb("mv", [P, T, 2])
        rstd = sb("rstd", [P, T])
        half = sb("half", [P, T])
        m_neg = sb("m_neg", [P, H])
        m_rest = sb("m_rest", [P, 2, H])
        m3 = sb("m3", [P, MR, H], BF16)
        m3T = sb("m3T", [MR * H, P], BF16)
        oS = sb("oS", [P, NQ, P])
        rden = sb("rden", [P, H])
        o = sb("o", [P, D])
        oT = sb("oT", [P, KC, P])
        stats2 = sb("stats2", [P, 6])
        mv2 = sb("mv2", [P, 2])
        rstd2 = sb("rstd2", [P, 1])
        pay = [sb(f"pay{i}", [P, PW]) for i in range(2)]
        dest = [sb(f"dest{i}", [P, 2], U32) for i in range(2)]
        x2T = sb("x2T", [P, KC, P])
        logit = sb("logit", [P, E])
        top = sb("top", [P, E])
        topi = sb("topi", [P, E], U32)
        topf = sb("topf", [P, 2])
        r1 = sb("r1", [P, 4])
        hot = sb("hot", [P, 3, E])
        hotb = sb("hotb", [P, E], BF16)
        iota8 = sb("iota8", [P, E])
        region0 = sb("region0", [P, E])
        count = sb("count", [P, E])
        pos = sb("pos", [P, 2, E])
        destf = sb("destf", [P, 2])
        tokid = sb("tokid", [P, 1])
        rowf = sb("rowf", [P, 1])
        nrow = sb("nrow", [P, E, 32])
        thr = sb("thr", [P, E, 32])
        ntile = sb("ntile", [P, E])
        ends = sb("ends", [P, E])
        jump = sb("jump", [P, E])
        iotaj = sb("iotaj", [P, TILES])
        past = sb("past", [P, TILES, E])
        jumps = sb("jumps", [P, TILES, E])
        tile_e = sb("tile_e", [P, TILES])
        tile_r = sb("tile_r", [P, TILES])
        tile_eu = sb("tile_eu", [P, TILES], U32)
        tile_ru = sb("tile_ru", [P, TILES], U32)
        padf = sb("padf", [P, E])
        padi = [sb(f"padi{e}", [P, 1], U32) for e in range(E)]
        zrow = sb("zrow", [P, PW])
        xf = [q3[:, i, :, :].rearrange("p a t -> p (a t)").bitcast(F32)[:, 0:PW] for i in range(2)]
        xfT = [xnT[:, i, 0:D].rearrange("p (c t) -> p c t", c=KC) for i in range(2)]
        hs = [qT[:, i, :] for i in range(2)]
        hT = [kT[:, i, :].rearrange("p (c t) -> p c t", c=FC) for i in range(2)]
        ys = [th[:, i, 0:D] for i in range(2)]
        ymeta = [sb(f"ymeta{i}", [P, 4]) for i in range(2)]
        ydest = [sb(f"ydest{i}", [P, 1], U32) for i in range(2)]
        fin = [[hid[:, 2 * i + s, :] for s in range(2)] for i in range(2)]

        banks = [ctx.enter_context(nc.psum_tensor(f"bank{i}", [P, 512], F32)) for i in range(8)]
        sq_bank, sk_bank, a_bank, o_bank, u_bank = banks[0:2], banks[2:4], banks[4:6], banks[6], banks[7]
        mT_ps = u_bank[0:MR * H, 0:P // 2].bitcast(BF16)

        c_wq, c_wk, c_wv, c_wo = sem("wq_loaded"), sem("wk_loaded"), sem("wv_loaded"), sem("wo_loaded")
        c_small = sem("small_loaded")
        c_x0, c_x = sem("x_first_loaded"), sem("x_rest_loaded")
        ctx_in = sem("ctx_loaded")
        w_exp = sem("expert_weights_loaded")
        const_pool, const_dve = sem("pool_constants"), sem("dve_constants")
        gelu_b, base_mm, base_ok = sem("wb1_gelu"), sem("base_product"), sem("base_ready")
        gates_ok = sem("gates_ready")
        ln_var, ln_rstd, xn_ok = sem("ln_variance"), sem("ln_rstd"), sem("xn_ready")
        a_done, a_free = sem("projection_done"), sem("projection_read")
        q3_ok, k3_ok = sem("q_parts_ready"), sem("k_parts_ready")
        qb, kb = sem("q_parts_stored"), sem("k_parts_stored")
        q_st, k_st = sem("q_stack_loaded"), sem("k_stack_loaded")
        s_done, max_done = sem("scores_done"), sem("max_done")
        m3_ok, mT_done, mT_sb, m_in = sem("max_parts"), sem("max_transposed"), sem("max_copied"), sem("max_rows_loaded")
        st_done, exp_done, pv_done = sem("shifted_scores_done"), sem("exp_done"), sem("pv_done")
        os_ok, nat_done, o_ok = sem("strips_copied"), sem("strips_transposed"), sem("o_ready")
        ot_done, ot_sb, op_done, y_ok = sem("o_transposed"), sem("oT_ready"), sem("out_projected"), sem("y_ready")
        l2_var, l2_rstd, x2_ok = sem("ln2_variance"), sem("ln2_rstd"), sem("x2_ready")
        x2t_done, x2t_sb = sem("x2_transposed"), sem("x2T_ready")
        lg_done, lg_read = sem("logits_done"), sem("logits_read")
        gap_ok, gap_exp = sem("gap_ready"), sem("gap_exp")
        hot_ok, cum_done, cum_read = sem("hot_ready"), sem("cum_done"), sem("cum_read")
        dest_ok = sem("dest_ready")
        sc = [sem("rows_sent_even"), sem("rows_sent_odd")]
        pad_ok, pad_in = sem("padding_index"), sem("padding_sent")
        table_ok = sem("tile_table")
        sp_passed, pool_passed, dve_passed, pe_passed = (sem(n) for n in ("sp_passed", "pool_passed", "dve_passed", "pe_passed"))
        dch, ach, pch = sem("dve_chain"), sem("act_chain"), sem("pool_chain")
        f_in = [sem("tile_loaded_even"), sem("tile_loaded_odd")]
        f_xt, f_xts = sem("tile_transposed"), sem("tile_xT_ready")
        f_h, f_hs = sem("hidden_done"), sem("hidden_silu")
        f_ht, f_hts = sem("hidden_transposed"), sem("hT_ready")
        f_y, f_ys = sem("tile_product"), sem("tile_scaled")
        f_out = sem("tile_sent")
        f_dest = sem("tile_dest")
        e_in = [sem("result_parts_even"), sem("result_parts_odd")]
        e_add = sem("result_added")
        e_out = sem("result_stored")

        block = ctx.enter_context(nc.Block())

        def head(par, side, h, t, rows):
            return stack[0:rows, par, side, h, t * P:(t + 1) * P]

        @block.sync
        def _(sp):
            sp.dma_start(xy[:, 0:T, :], x_t[:, 0:T, :]).then_inc(c_x0, 16)
            sp.dma_start(ctxg[:], ctx_t[:, :, 0:GT]).then_inc(ctx_in, 16)
            for w_sb, w, c in ((wq_sb, wqT, c_wq), (wk_sb, wkT, c_wk)):
                sp.dma_start(w_sb[:], w.rearrange("(c p) n -> p c n", p=P)).then_inc(c, 16)
            small = (
                (wb1_sb[:], wb1), (wb2_sb[:], wb2T), (g1_sb[:], gate1), (g2_sb[:], gate2),
                (mask_u[:, 0, :], mask), (mask_u[:, 1, :], maskT),
                (graw[:, 0:1], gx.broadcast_to([P, 1])), (graw[:, 1:2], gf.broadcast_to([P, 1])),
                (wr_sb[:], wr.rearrange("(c p) e -> p c e", p=P)),
            )
            assert len(small) == SMALL
            for to, of in small:
                sp.dma_start(to, of).then_inc(c_small, 16)
            for w_sb, w, c in ((wv_sb, wvT, c_wv), (wo_sb, woT, c_wo)):
                sp.dma_start(w_sb[:], w.rearrange("(c p) n -> p c n", p=P)).then_inc(c, 16)
            sp.dma_start(xy[:, T:B, :], x_t[:, T:B, :]).then_inc(c_x, 16)

            def store_parts(g, first, ready, stored, loaded, parts, dram):
                sp.wait_ge(ready, g + 1)
                sp.sem_inc(sp_passed, 1)
                if not first:
                    sp.wait_ge(loaded, 16 * NT * g)
                sp.dma_start(dram.rearrange("(c p) s t -> p c s t", p=P), parts[:]).then_inc(stored, 16)

            def load_stack(g, par, stored, loaded, dram, side, terms):
                sp.wait_ge(stored, 16 * (g + 1))
                for j, part in enumerate(terms):
                    sp.dma_start(stack[DH * j:DH * (j + 1), par, side, :, :],
                                 dram[:, part, :].rearrange("(h d) t -> d h t", d=DH)).then_inc(loaded, 16)

            def load_max(n, par, t):
                sp.wait_ge(mT_sb, n + 1)
                for i in range(MR):
                    sp.dma_start(stack[KR + i:KR + i + 1, par, 0, :, t * P:(t + 1) * P],
                                 m3T[H * i:H * (i + 1), :]).then_inc(m_in, 16)

            store_parts(0, True, k3_ok, kb, k_st, k3, kparts_d)
            load_stack(0, 0, kb, k_st, kparts_d, 1, TERMS_K)
            store_parts(0, True, q3_ok, qb, q_st, q3, qparts_d)
            load_stack(0, 0, qb, q_st, qparts_d, 0, TERMS_Q)
            load_max(0, 0, 0)

            def group(g, par, last):
                n = T * g
                if not last:
                    sp.wait_ge(a_done, A_USES * (g + 1))
                    sp.dma_start(ctxg[:], ctx_t[:, :, bass.ds((g + 1) * GT, GT)]).then_inc(ctx_in, 16)
                load_max(n + 1, par, 1)
                load_max(n + 2, par, 2)
                if not last:
                    store_parts(g + 1, False, k3_ok, kb, k_st, k3, kparts_d)
                    load_stack(g + 1, 1 - par, kb, k_st, kparts_d, 1, TERMS_K)
                    store_parts(g + 1, False, q3_ok, qb, q_st, q3, qparts_d)
                    load_stack(g + 1, 1 - par, qb, q_st, qparts_d, 0, TERMS_Q)
                load_max(n + 3, par, 3)
                if not last:
                    load_max(n + 4, 1 - par, 0)

            group(0, 0, False)
            with sp.Fori(0, (G - 2) // 2) as gg:
                group(2 * gg + 1, 1, False)
                group(2 * gg + 2, 0, False)
            group(G - 1, 1, True)
            sp.wait_ge(st_done, NQ * B)
            for e in range(E):
                sp.dma_start(w2_sb[:, e, :, :], w2[e, :, :].rearrange("(c p) f -> p c f", p=P)).then_inc(w_exp, 16)

            sp.wait_ge(table_ok, 1)
            sp.wait_ge(sc[0], 32 * B // 2)
            sp.wait_ge(sc[1], 32 * B // 2)
            sp.wait_ge(pad_in, 16 * (E + SPARE))

            def load_tile(j, i, first):
                row = sp.value_load(tile_ru[0:1, bass.ds(j, 1)], min_val=0, max_val=E * REGION + (SPARE - 1) * P)
                if not first:
                    sp.wait_ge(f_ys, j - 1)
                sp.dma_start(xf[i], rows_d[bass.ds(row, P), :]).then_inc(f_in[i], 16)

            load_tile(0, 0, True)
            load_tile(1, 1, True)
            with sp.Fori(1, TILES // 2) as jj:
                load_tile(2 * jj, 0, False)
                load_tile(2 * jj + 1, 1, False)

            sp.wait_ge(f_out, 16 * TILES)

            def load_result(k, i, first):
                if not first:
                    sp.wait_ge(e_add, k - 1)
                    sp.sem_inc(sp_passed, 1)
                for s in range(2):
                    sp.dma_start(fin[i][s].rearrange("p (u d) -> p u d", d=D),
                                 ffn_d[bass.ds(s * REGION + k * 2 * P, 2 * P), :].rearrange("(u p) d -> p u d", p=P))\
                        .then_inc(e_in[i], 16)

            def store_result(k):
                sp.wait_ge(e_add, k + 1)
                sp.sem_inc(sp_passed, 1)
                sp.dma_start(out_t[:, bass.ds(2 * k, 2), :], xy[:, bass.ds(2 * k, 2), :]).then_inc(e_out, 16)

            load_result(0, 0, True)
            load_result(1, 1, True)
            with sp.Fori(1, B // 4) as kk:
                store_result(2 * kk - 2)
                load_result(2 * kk, 0, False)
                store_result(2 * kk - 1)
                load_result(2 * kk + 1, 1, False)
            store_result(B // 2 - 2)
            store_result(B // 2 - 1)
            sp.wait_ge(e_out, 16 * (B // 2))

        @block.gpsimd
        def _(pool):
            nc.gpsimd.memset(ident[:], 0.0).then_inc(const_pool, 1)
            nc.gpsimd.memset(identb[:], 0.0).then_inc(const_pool, 1)
            nc.gpsimd.memset(before[:], 1.0).then_inc(const_pool, 1)
            pool.wait_ge(const_pool, 3)
            for m in (ident, identb):
                nc.gpsimd.affine_select(out=m[:], in_=m[:], compare_op=ALU.not_equal, fill=1.0, base=0,
                                        pattern=[[-1, P]], channel_multiplier=1).then_inc(const_pool, 1)
            nc.gpsimd.affine_select(out=before[:], in_=before[:], compare_op=ALU.is_gt, fill=0.0, base=0,
                                    pattern=[[1, P]], channel_multiplier=-1).then_inc(const_pool, 1)
            nc.gpsimd.memset(half[:], -0.5).then_inc(const_pool, 1)
            nc.gpsimd.memset(v[:], 0.0).then_inc(const_pool, 1)
            pool.wait_ge(const_pool, 8)
            nc.gpsimd.memset(v[:, :, :, DH:DH + 1], 1.0).then_inc(const_pool, 1)
            nc.gpsimd.iota(iota8[:], pattern=[[1, E]], base=0, channel_multiplier=0,
                           allow_small_or_imprecise_dtypes=True).then_inc(const_pool, 1)
            nc.gpsimd.iota(region0[:], pattern=[[REGION, E]], base=0, channel_multiplier=0,
                           allow_small_or_imprecise_dtypes=True).then_inc(const_pool, 1)
            nc.gpsimd.iota(tokid[:], pattern=[[0, 1]], base=0, channel_multiplier=1,
                           allow_small_or_imprecise_dtypes=True).then_inc(const_pool, 1)
            nc.gpsimd.iota(thr[:], pattern=[[0, E], [P, 32]], base=0, channel_multiplier=0,
                           allow_small_or_imprecise_dtypes=True).then_inc(const_pool, 1)
            nc.gpsimd.iota(iotaj[:], pattern=[[1, TILES]], base=0, channel_multiplier=0,
                           allow_small_or_imprecise_dtypes=True).then_inc(const_pool, 1)
            nc.gpsimd.memset(zrow[:], 0.0).then_inc(const_pool, 1)
            nc.gpsimd.memset(count[:], 0.0).then_inc(const_pool, 1)
            nc.gpsimd.iota(rowf[:], pattern=[[0, 1]], base=0, channel_multiplier=1,
                           allow_small_or_imprecise_dtypes=True).then_inc(const_pool, 1)
            pool.wait_ge(const_pool, CONST_POOL - 1)
            nc.gpsimd.iota(zrow[:, PW - 1:PW], pattern=[[0, 1]], base=TOK, channel_multiplier=1,
                           allow_small_or_imprecise_dtypes=True).then_inc(const_pool, 1)
            pool.wait_ge(const_pool, CONST_POOL)
            for i in range(SPARE):
                pool.dma_start(rows_d[PAD_ROWS + i * P:PAD_ROWS + (i + 1) * P, :], zrow[:]).then_inc(pad_in, 16)

            def rstd_of(g):
                pool.wait_ge(ln_var, g + 1)
                nc.gpsimd.tensor_tensor(rstd[:], mv[:, :, 1], half[:], ALU.pow).then_inc(ln_rstd, 1)

            def split_k(g, first):
                pool.wait_ge(a_free, A_USES * g + KC)
                if not first:
                    pool.wait_ge(kb, 16 * g)
                for c in range(KC):
                    w = (4 * KC - 1) * g + 4 * c
                    pool.sem_inc(pool_passed, 1)
                    nc.gpsimd.tensor_copy(k3[:, c, 0, :], kT[:, c, :]).then_inc(pch, 1)
                    pool.wait_ge(pch, w + 1)
                    nc.gpsimd.tensor_tensor(krest[:], kT[:, c, :], k3[:, c, 0, :], ALU.subtract).then_inc(pch, 1)
                    pool.wait_ge(pch, w + 2)
                    pool.sem_inc(pool_passed, 1)
                    nc.gpsimd.tensor_copy(k3[:, c, 1, :], krest[:]).then_inc(pch, 1)
                    pool.wait_ge(pch, w + 3)
                    last = nc.gpsimd.tensor_tensor(k3[:, c, 2, :], krest[:], k3[:, c, 1, :], ALU.subtract)
                    if c < KC - 1:
                        last.then_inc(pch, 1)
                        pool.wait_ge(pch, w + 4)
                last.then_inc(k3_ok, 1)

            def rstd2_of(r):
                pool.wait_ge(l2_var, r + 1)
                nc.gpsimd.tensor_tensor(rstd2[:], mv2[:, 1:2], half[:, 0:1], ALU.pow).then_inc(l2_rstd, 1)

            def send(r, i):
                pool.wait_ge(dest_ok, r + 1)
                pool.sem_inc(pool_passed, 1)
                for s in range(2):
                    pool.indirect_dma_start(rows_d, bass.IndirectOffsetOnAxis(ap=dest[i][:, s:s + 1], axis=0),
                                            pay[i][:], None).then_inc(sc[i], 16)

            rstd_of(0)
            split_k(0, True)

            def group(g, first, last):
                for t in range(T):
                    n = T * g + t
                    if not (first and t < 3):
                        send(n - 3, (t + 1) % 2)
                    if not (first and t < 2):
                        rstd2_of(n - 2)
                    if t == 0 and not last:
                        rstd_of(g + 1)
                    if t == 1 and not last:
                        split_k(g + 1, False)

            group(0, True, False)
            with pool.Fori(1, G - 1) as g:
                group(g, False, False)
            group(G - 1, False, True)
            for n in (B, B + 1):
                send(n - 3, (n + 1) % 2)
                rstd2_of(n - 2)
            send(B - 1, 1)
            pool.wait_ge(pad_ok, 1)
            for e in range(E):
                pool.indirect_dma_start(rows_d, bass.IndirectOffsetOnAxis(ap=padi[e][:, 0:1], axis=0),
                                        zrow[:], None).then_inc(pad_in, 16)

            def send_tile(j, i, first):
                pool.wait_ge(f_ys, j + 1)
                if not first:
                    pool.wait_ge(f_out, 16 * j)
                    pool.sem_inc(pool_passed, 1)
                pool.indirect_dma_start(ffn_d, bass.IndirectOffsetOnAxis(ap=ydest[i][:, 0:1], axis=0),
                                        ys[i], None).then_inc(f_out, 16)

            send_tile(0, 0, True)
            send_tile(1, 1, False)
            with pool.Fori(1, TILES // 2) as jj:
                send_tile(2 * jj, 0, False)
                send_tile(2 * jj + 1, 1, False)

        @block.scalar
        def _(act):
            act.wait_ge(c_small, 16 * SMALL)
            nc.scalar.activation(wb1g[:], wb1_sb[:], ACT.Gelu, scale=math.log(N_CONTEXT)).then_inc(gelu_b, 1)
            nc.scalar.activation(gates[:], graw[:], ACT.Tanh).then_inc(gates_ok, 1)

            def evac(g, u, to, func=None):
                act.wait_ge(a_done, A_USES * g + u + 1)
                nc.scalar.activation(to, a_bank[u % 2][:, 0:to_width(to)], func or ACT.Copy).then_inc(a_free, 1)

            def to_width(to):
                return math.prod(to.shape[1:])

            def stage_kq(g, first):
                if not first:
                    act.wait_ge(k3_ok, g)
                for c in range(KC):
                    evac(g, c, kT[:, c, :])
                for c in range(KC):
                    evac(g, 2 + c, xnT[:, c, :])
                if not first:
                    act.wait_ge(q3_ok, g)
                for c in range(KC):
                    evac(g, 4 + c, qT[:, c, :])
                stage_gate(g, 0, 6)

            def stage_gate(g, c, u):
                for p in range(PAIRS):
                    evac(g, u + p, hid[:, p, :], ACT.Gelu)
                evac(g, u + PAIRS, th[:, c, :], ACT.Tanh)

            def stage_v(g):
                for t in range(T):
                    act.wait_ge(a_done, A_USES * g + 16 + t + 1)
                    nc.scalar.activation(v[:, t, :, 0:DH],
                                         a_bank[t % 2][:, 0:D].rearrange("p (h d) -> p h d", d=DH),
                                         ACT.Copy).then_inc(a_free, 1)

            def copy_max(n, first):
                act.wait_ge(mT_done, n + 1)
                if not first:
                    act.wait_ge(m_in, 16 * MR * n)
                nc.scalar.activation(m3T[:], mT_ps, ACT.Copy).then_inc(mT_sb, 1)

            stage_kq(0, True)
            stage_gate(0, 1, 11)
            act.wait_ge(const_pool, CONST_POOL)
            stage_v(0)
            copy_max(0, True)

            def slot(g, t, a, scores, nxt, old1, old2):
                n = T * g + t
                if old1:
                    act.wait_ge(pv_done, NQ * n)
                    if old2:
                        act.wait_ge(nat_done, n - 1)
                    nc.scalar.activation(oS[:].rearrange("p c q -> p (c q)"), o_bank[:], ACT.Copy).then_inc(os_ok, 1)
                for c in range(NQ):
                    if scores:
                        act.wait_ge(st_done, NQ * n + c + 1)
                        if old1:
                            act.wait_ge(pv_done, NQ * (n - 1) + c + 1)
                        nc.scalar.activation(pT[:, c, :], sk_bank[c % 2][:], ACT.Exp).then_inc(exp_done, 1)
                    if c == 1 and old2:
                        act.wait_ge(x2t_done, n - 1)
                        nc.scalar.activation(x2T[:].rearrange("p c t -> p (c t)"), u_bank[:, 0:D], ACT.Copy)\
                            .then_inc(x2t_sb, 1)
                    if c == 2 and old1:
                        act.wait_ge(ot_done, n)
                        nc.scalar.activation(oT[:].rearrange("p c t -> p (c t)"), u_bank[:, 0:D], ACT.Copy)\
                            .then_inc(ot_sb, 1)
                if old2:
                    act.wait_ge(gap_ok, n - 1)
                    nc.scalar.activation(r1[:, 1:2], r1[:, 0:1], ACT.Exp).then_inc(gap_exp, 1)
                if nxt:
                    copy_max(n + 1, False)
                if a and t == 0:
                    stage_kq(g + 1, False)
                if a and t == 1:
                    stage_gate(g + 1, 1, 11)
                if a and t == 3:
                    stage_v(g + 1)

            for t in range(T):
                slot(0, t, True, True, True, t >= 1, t >= 2)
            with act.Fori(1, G - 1) as g:
                for t in range(T):
                    slot(g, t, True, True, True, True, True)
            act.wait_ge(st_done, NQ * T * (G - 1))
            for e in range(E):
                act.dma_start(w1_sb[:, e, :, :], w1[e, :, :].rearrange("(c p) f -> p c f", p=P)).then_inc(w_exp, 16)
            for t in range(T):
                slot(G - 1, t, False, True, t < T - 1, True, True)
            slot(G, 0, False, False, False, True, True)
            slot(G, 1, False, False, False, False, True)

            def tile_in(j, i, first):
                act.wait_ge(f_xt, j + 1)
                nc.scalar.activation(xfT[i].rearrange("p c t -> p (c t)"), banks[i][:, 0:D], ACT.Copy).then_inc(f_xts, 1)
                act.wait_ge(f_h, j + 1)
                if not first:
                    act.wait_ge(f_ht, j - 1)
                nc.scalar.activation(hs[i], banks[2 + i][:], ACT.Silu).then_inc(f_hs, 1)

            tile_in(0, 0, True)
            tile_in(1, 1, True)
            with act.Fori(1, TILES // 2) as jj:
                tile_in(2 * jj, 0, False)
                tile_in(2 * jj + 1, 1, False)

        @block.vector
        def _(dve):
            chain = [0, 0]

            def link(ins):
                chain[0] += 1
                ins.then_inc(dch, 1)
                dve.wait_ge(dch, chain[1] + chain[0])


            def layer_norm_stats(g):
                for t in range(T):
                    link(nc.vector.bn_stats(stats[:, t, :], xy[:, T * g + t, :]))
                for t in range(T):
                    dve.sem_inc(dve_passed, 1)
                    link(nc.vector.bn_aggr(mv[:, t, :], stats[:, t, :]))
                nc.vector.tensor_scalar(mv[:, :, 1], mv[:, :, 1], EPS, None, ALU.add).then_inc(ln_var, 1)

            def layer_norm(g, first):
                dve.wait_ge(ln_rstd, g + 1)
                if not first:
                    dve.wait_ge(a_done, A_USES * (g - 1) + 4)
                for t in range(T):
                    ins = nc.vector.tensor_scalar(xn[:, t, :], xy[:, T * g + t, :], mv[:, t, 0:1], rstd[:, t:t + 1],
                                                  ALU.subtract, ALU.mult)
                ins.then_inc(xn_ok, 1)

            def q_parts(g, c, first):
                dve.wait_ge(a_free, A_USES * g + (11 if c == 0 else 16))
                if not first and c == 0:
                    dve.wait_ge(qb, 16 * g)
                link(nc.vector.tensor_scalar(rest[:], qT[:, c, :], base[:, c:c + 1], None, ALU.mult))
                link(nc.vector.scalar_tensor_tensor(qT[:, c, :], th[:, c, :], 1.0, rest[:], ALU.add, ALU.mult))
                link(nc.vector.tensor_copy(q3[:, c, 0, :], qT[:, c, :]))
                link(nc.vector.tensor_tensor(rest[:], qT[:, c, :], q3[:, c, 0, :], ALU.subtract))
                link(nc.vector.tensor_copy(q3[:, c, 1, :], rest[:]))
                ins = nc.vector.tensor_tensor(q3[:, c, 2, :], rest[:], q3[:, c, 1, :], ALU.subtract)
                if c == 0:
                    link(ins)
                else:
                    ins.then_inc(q3_ok, 1)

            def row_max(n, c):
                dve.wait_ge(s_done, NQ * n + c + 1)
                nc.vector.tensor_reduce(m_neg[:, QH * c:QH * (c + 1)],
                                        sq_bank[c % 2][:].rearrange("p (h k) -> p h k", h=QH),
                                        axis=AX.X, op=ALU.max, negate=True).then_inc(max_done, 1)

            def max_parts(n, first):
                dve.wait_ge(max_done, NQ * (n + 1))
                if not first:
                    dve.wait_ge(mT_done, n)
                link(nc.vector.tensor_copy(m3[:, 0, :], m_neg[:]))
                link(nc.vector.tensor_tensor(m_rest[:, 0, :], m_neg[:], m3[:, 0, :], ALU.subtract))
                link(nc.vector.tensor_copy(m3[:, 1, :], m_rest[:, 0, :]))
                nc.vector.tensor_tensor(m3[:, 2, :], m_rest[:, 0, :], m3[:, 1, :], ALU.subtract).then_inc(m3_ok, 1)

            dve.wait_ge(c_x0, 16)
            layer_norm_stats(0)
            layer_norm(0, True)
            dve.wait_ge(c_small, 16 * SMALL)
            link(nc.vector.tensor_scalar(bias_b[:], mask_u[:], -NEG, NEG, ALU.mult, ALU.add))
            link(nc.vector.tensor_reduce(seen[:, 0:1], mask_u[:, 0, :], axis=AX.X, op=ALU.max))
            link(nc.vector.reciprocal(seen[:, 1:2], seen[:, 0:1]))
            link(nc.vector.tensor_tensor(seen[:, 2:3], seen[:, 0:1], seen[:, 1:2], ALU.mult))
            dve.wait_ge(gates_ok, 1)
            nc.vector.tensor_tensor(seen[:, 3:4], seen[:, 2:3], gates[:, 0:1], ALU.mult).then_inc(const_dve, 1)
            dve.wait_ge(base_mm, 1)
            link(nc.vector.tensor_scalar(base[:], o_bank[:, 0:KC], DH ** -0.5, None, ALU.mult))
            q_parts(0, 0, True)
            q_parts(0, 1, True)
            nc.vector.memset(ones_b[:], 1.0).then_inc(const_dve, 1)
            nc.vector.memset(stack[KR:KR + MR, :, 1, :, :].bitcast(F32), TWO_ONES).then_inc(const_dve, 1)
            for c in range(NQ):
                row_max(0, c)
            max_parts(0, True)

            dve.wait_ge(const_pool, CONST_POOL)
            dve.wait_ge(const_dve, 3)

            def slot(g, t, a, nxt, old1, old2, old3):
                n = T * g + t
                if old3:
                    destinations(n - 3, (t + 1) % 2)
                if old2:
                    link(nc.vector.bn_stats(stats2[:], xy[:, n - 2, :]))
                    dve.sem_inc(dve_passed, 1)
                    link(nc.vector.bn_aggr(mv2[:], stats2[:]))
                    nc.vector.tensor_scalar(mv2[:, 1:2], mv2[:, 1:2], EPS, None, ALU.add).then_inc(l2_var, 1)
                for c in range(NQ):
                    if nxt:
                        row_max(n + 1, c)
                    if c == 0 and old2:
                        normalise2(g, n - 2, t % 2, (2 * g + t // 2 - 1), old2 == 2)
                    if c == 0 and old1:
                        dve.wait_ge(nat_done, n)
                        if old2:
                            dve.wait_ge(ot_done, n - 1)
                        strips = u_bank[:].rearrange("p (h w) -> p h w", w=VW)
                        link(nc.vector.reciprocal(rden[:], strips[:, :, DH]))
                        nc.vector.tensor_tensor(o[:].rearrange("p (h d) -> p h d", d=DH), strips[:, :, 0:DH],
                                                rden[:].unsqueeze(2).to_broadcast([P, H, DH]), ALU.mult).then_inc(o_ok, 1)
                    if c == 0 and a and t == 0:
                        layer_norm_stats(g + 1)
                    if c == 1 and a and t == 0:
                        layer_norm(g + 1, False)
                    if c == 1 and a and t == 1:
                        q_parts(g + 1, 0, False)
                    if c == 1 and a and t == 2:
                        q_parts(g + 1, 1, False)
                if nxt:
                    max_parts(n + 1, False)
                if old2:
                    route(n - 2, t % 2)
                if old1:
                    dve.wait_ge(op_done, n)
                    nc.vector.scalar_tensor_tensor(xy[:, n - 1, :], u_bank[:, 0:D], seen[:, 3:4], xy[:, n - 1, :],
                                                   ALU.mult, ALU.add).then_inc(y_ok, 1)
                    dve.wait_ge(y_ok, n)

            def normalise2(g, r, i, kth, reused):
                dve.wait_ge(l2_rstd, r + 1)
                if reused:
                    dve.wait_ge(sc[i], 32 * kth)
                nc.vector.tensor_scalar(pay[i][:, 0:D], xy[:, r, :], mv2[:, 0:1], rstd2[:, 0:1],
                                        ALU.subtract, ALU.mult).then_inc(x2_ok, 1)

            def route(r, i):
                dve.wait_ge(lg_done, r + 1)
                nc.vector.tensor_copy(logit[:], u_bank[:, 0:E]).then_inc(lg_read, 1)
                dve.wait_ge(lg_read, r + 1)
                dve.sem_inc(dve_passed, 1)
                link(nc.vector.max(top[:], logit[:]))
                nc.vector.tensor_tensor(r1[:, 0:1], top[:, 1:2], top[:, 0:1], ALU.subtract).then_inc(gap_ok, 1)
                link(nc.vector.max_index(topi[:], top[:], logit[:]))
                link(nc.vector.tensor_copy(topf[:], topi[:, 0:2]))
                nc.vector.tensor_copy(pay[i][:, D + 2:D + 3], topf[:, 0:1])
                for s in range(2):
                    link(nc.vector.tensor_scalar(hot[:, s, :], iota8[:], topf[:, s:s + 1], None, ALU.is_equal))
                nc.vector.tensor_tensor(hotb[:], hot[:, 0, :], hot[:, 1, :], ALU.add).then_inc(hot_ok, 1)
                dve.wait_ge(gap_exp, r + 1)
                link(nc.vector.tensor_scalar(r1[:, 2:3], r1[:, 1:2], 1.0, None, ALU.add))
                link(nc.vector.reciprocal(r1[:, 3:4], r1[:, 2:3]))
                link(nc.vector.tensor_scalar(pay[i][:, D:D + 1], r1[:, 3:4], gates[:, 1:2], None, ALU.mult))
                link(nc.vector.tensor_tensor(pay[i][:, D + 1:D + 2], pay[i][:, D:D + 1], r1[:, 1:2], ALU.mult))
                nc.vector.tensor_copy(pay[i][:, D + 3:D + 4], tokid[:])
                link(nc.vector.tensor_scalar(tokid[:], tokid[:], float(S), None, ALU.add))

            def destinations(r, i):
                dve.wait_ge(cum_done, r + 1)
                link(nc.vector.tensor_tensor(pos[:, 0, :], u_bank[:, 0:E], count[:], ALU.add))
                nc.vector.tensor_tensor(count[:], u_bank[:, E:2 * E], count[:], ALU.add).then_inc(cum_read, 1)
                dve.wait_ge(cum_read, r + 1)
                link(nc.vector.tensor_tensor(pos[:, 0, :], pos[:, 0, :], region0[:], ALU.add))
                for s in range(2):
                    link(nc.vector.tensor_tensor(pos[:, 1, :], pos[:, 0, :], hot[:, s, :], ALU.mult))
                    link(nc.vector.tensor_reduce(destf[:, s:s + 1], pos[:, 1, :], axis=AX.X, op=ALU.add))
                nc.vector.tensor_copy(dest[i][:], destf[:]).then_inc(dest_ok, 1)

            dve.wait_ge(c_x, 16)
            for t in range(T):
                slot(0, t, True, True, t >= 1, t >= 2, t >= 3)
            first_links = chain[0]
            with dve.Fori(1, G - 1) as g:
                chain[:] = [0, first_links + (g - 1) * LINKS]
                for t in range(T):
                    slot(g, t, True, True, True, 2, True)
                assert chain[0] == LINKS, chain[0]
            chain[:] = [0, first_links + (G - 2) * LINKS]
            for t in range(T):
                slot(G - 1, t, False, t < T - 1, True, 2, True)
            slot(G, 0, False, False, True, 2, True)
            slot(G, 1, False, False, False, 2, True)
            destinations(B - 1, 1)

            link(nc.vector.tensor_tensor(padf[:], count[:], region0[:], ALU.add))
            link(nc.vector.tensor_scalar(padf[:], padf[:], rowf[:, 0:1], None, ALU.add))
            for e in range(E):
                ins = nc.vector.tensor_copy(padi[e][:], padf[:, e:e + 1])
            ins.then_inc(pad_ok, 1)
            link(nc.vector.tensor_tensor(nrow[:], count[:].unsqueeze(2).to_broadcast([P, E, 32]), thr[:], ALU.is_gt))
            link(nc.vector.tensor_reduce(ntile[:], nrow[:], axis=AX.X, op=ALU.add))
            link(nc.vector.tensor_copy(ends[:, 0:1], ntile[:, 0:1]))
            for e in range(1, E):
                link(nc.vector.tensor_tensor(ends[:, e:e + 1], ends[:, e - 1:e], ntile[:, e:e + 1], ALU.add))
            link(nc.vector.tensor_scalar(jump[:], ntile[:], -float(P), float(REGION), ALU.mult, ALU.add))
            link(nc.vector.tensor_tensor(past[:], iotaj[:].unsqueeze(2).to_broadcast([P, TILES, E]),
                                         ends[:].unsqueeze(1).to_broadcast([P, TILES, E]), ALU.is_ge))
            link(nc.vector.tensor_tensor(jumps[:], past[:], jump[:].unsqueeze(1).to_broadcast([P, TILES, E]), ALU.mult))
            link(nc.vector.tensor_reduce(tile_e[:], past[:], axis=AX.X, op=ALU.add))
            link(nc.vector.tensor_scalar(tile_e[:], tile_e[:], float(E - 1), None, ALU.min))
            link(nc.vector.tensor_reduce(tile_r[:], jumps[:], axis=AX.X, op=ALU.add))
            link(nc.vector.scalar_tensor_tensor(tile_r[:], iotaj[:], float(P), tile_r[:], ALU.mult, ALU.add))
            link(nc.vector.tensor_copy(tile_eu[:], tile_e[:]))
            nc.vector.tensor_copy(tile_ru[:], tile_r[:]).then_inc(table_ok, 1)
            dve.wait_ge(table_ok, 1)

            def tile(j, i, jj, first, base_):
                chain[:] = [0, base_]
                dve.wait_ge(f_in[i], 16 * (jj + 1))
                if not first:
                    dve.wait_ge(f_out, 16 * (j - 1))
                link(nc.vector.tensor_tensor(ymeta[i][:, 0:1], tile_e[:, bass.ds(j, 1)], xf[i][:, D + 2:D + 3], ALU.is_equal))
                link(nc.vector.tensor_tensor(ymeta[i][:, 1:2], xf[i][:, D:D + 1], xf[i][:, D + 1:D + 2], ALU.subtract))
                link(nc.vector.scalar_tensor_tensor(ymeta[i][:, 2:3], ymeta[i][:, 1:2], ymeta[i][:, 0:1], xf[i][:, D + 1:D + 2],
                                                    ALU.mult, ALU.add))
                link(nc.vector.tensor_scalar(ymeta[i][:, 3:4], ymeta[i][:, 0:1], -float(REGION), float(REGION),
                                             ALU.mult, ALU.add))
                link(nc.vector.tensor_tensor(ydest[i][:], ymeta[i][:, 3:4], xf[i][:, D + 3:D + 4], ALU.add))
                dve.wait_ge(f_ht, j + 1)
                nc.vector.tensor_copy(hT[i].rearrange("p c t -> p (c t)"), banks[4 + i][:]).then_inc(f_hts, 1)
                dve.wait_ge(f_y, j + 1)
                nc.vector.tensor_scalar(ys[i], banks[6 + i][:, 0:D], ymeta[i][:, 2:3], None, ALU.mult).then_inc(f_ys, 1)

            links0 = chain[0] + first_links + (G - 2) * LINKS
            tile(0, 0, 0, True, links0)
            tile(1, 1, 0, True, links0 + 5)
            with dve.Fori(1, TILES // 2) as jj:
                tile(2 * jj, 0, jj, False, links0 + 10 * jj)
                tile(2 * jj + 1, 1, jj, False, links0 + 10 * jj + 5)

            def result(k, i, kk):
                dve.wait_ge(e_in[i], 32 * (kk + 1))
                y2 = xy[:, bass.ds(2 * k, 2), :].rearrange("p u d -> p (u d)")
                nc.vector.tensor_tensor(y2, y2, fin[i][0], ALU.add).then_inc(dch, 1)
                dve.wait_ge(dch, links1 + k + 1)
                nc.vector.tensor_tensor(y2, y2, fin[i][1], ALU.add).then_inc(e_add, 1)

            links1 = links0 + 5 * TILES
            with dve.Fori(0, B // 4) as kk:
                result(2 * kk, 0, kk)
                result(2 * kk + 1, 1, kk)

        def rowid():
            return rowf[:, 0:1]

        @block.tensor
        def _(pe):
            def use(g, u):
                if not isinstance(g, int) or A_USES * g + u >= 2:
                    pe.wait_ge(a_free, A_USES * g + u - 1)
                return a_bank[u % 2]

            def stage_kq(g):
                pe.wait_ge(ctx_in, 16 * (g + 1))
                for m in range(KC):
                    bank = use(g, m)
                    for c in range(KC):
                        last = nc.tensor.matmul(bank[:], wk_sb[:, c, m * P:(m + 1) * P], ctxg[:, c, :],
                                                start=c == 0, stop=c == KC - 1)
                    last.then_inc(a_done, 1)
                pe.wait_ge(xn_ok, g + 1)
                for c in range(KC):
                    bank = use(g, 2 + c)
                    for t in range(T):
                        last = nc.tensor.transpose(bank[:, t * P:(t + 1) * P], xn[:, t, c * P:(c + 1) * P], ident[:])
                    last.then_inc(a_done, 1)
                pe.wait_ge(a_free, A_USES * g + 4)
                for m in range(KC):
                    bank = use(g, 4 + m)
                    for c in range(KC):
                        last = nc.tensor.matmul(bank[:], wq_sb[:, c, m * P:(m + 1) * P], xnT[:, c, :],
                                                start=c == 0, stop=c == KC - 1)
                    last.then_inc(a_done, 1)
                stage_gate(g, 0, 6)

            def stage_gate(g, c, u):
                pe.wait_ge(a_free, A_USES * g + 6)
                for p in range(PAIRS):
                    bank = use(g, u + p)
                    nc.tensor.matmul(bank[:], g1_sb[:, p, :], qT[:, c, :], start=True, stop=True).then_inc(a_done, 1)
                bank = use(g, u + PAIRS)
                for p in range(PAIRS):
                    pe.wait_ge(a_free, A_USES * g + u + p + 1)
                    last = nc.tensor.matmul(bank[2 * DH * p:2 * DH * (p + 1), :], g2_sb[:], hid[:, p, :],
                                            start=True, stop=True)
                last.then_inc(a_done, 1)

            def stage_v(g):
                for t in range(T):
                    bank = use(g, 16 + t)
                    for c in range(KC):
                        last = nc.tensor.matmul(bank[:, 0:D], ctxg[:, c, t * P:(t + 1) * P], wv_sb[:, c, :],
                                                start=c == 0, stop=c == KC - 1)
                    last.then_inc(a_done, 1)

            def bias(bank, side):
                nc.tensor.matmul(bank[:], identb[:], bias_b[:, side, :].unsqueeze(1).to_broadcast([P, QH, P]),
                                 start=True, stop=False)

            def scores(n, g, par, t, c):
                if not isinstance(n, int) or NQ * n + c >= 2:
                    pe.wait_ge(max_done, NQ * n + c - 1)
                if c == 0 and t == 0:
                    pe.wait_ge(q_st, 16 * NT * (g + 1))
                    pe.wait_ge(k_st, 16 * NT * (g + 1))
                bank = sq_bank[c % 2]
                bias(bank, 0)
                for j in range(QH):
                    h = QH * c + j
                    last = nc.tensor.matmul(bank[:, j * P:(j + 1) * P], head(par, 0, h, t, KR),
                                            head(par, 1, h, t, KR), start=False, stop=j == QH - 1)
                last.then_inc(s_done, 1)

            def shifted(n, par, t, c):
                if not isinstance(n, int) or NQ * n + c >= 2:
                    pe.wait_ge(exp_done, NQ * n + c - 1)
                if c == 0:
                    pe.wait_ge(m_in, 16 * MR * (n + 1))
                bank = sk_bank[c % 2]
                bias(bank, 1)
                for j in range(QH):
                    h = QH * c + j
                    last = nc.tensor.matmul(bank[:, j * P:(j + 1) * P], head(par, 1, h, t, KR + MR),
                                            head(par, 0, h, t, KR + MR), start=False, stop=j == QH - 1)
                last.then_inc(st_done, 1)

            def values(n, t, c, old1):
                pe.wait_ge(exp_done, NQ * n + c + 1)
                if c == 0 and old1:
                    pe.wait_ge(os_ok, n)
                for j in range(QH):
                    last = nc.tensor.matmul(o_bank[VW * j:VW * (j + 1), c * P:(c + 1) * P], v[:, t, QH * c + j, :],
                                            pT[:, c, j * P:(j + 1) * P], start=True, stop=True)
                last.then_inc(pv_done, 1)

            def max_rows(n):
                pe.wait_ge(m3_ok, n + 1)
                pe.sem_inc(pe_passed, 1)
                nc.tensor.transpose(mT_ps, m3[:].rearrange("p s h -> p (s h)"), identb[:]).then_inc(mT_done, 1)

            pe.wait_ge(gelu_b, 1)
            for c in range(KC):
                last = nc.tensor.matmul(o_bank[:, c:c + 1], wb2_sb[:, c * P:(c + 1) * P], wb1g[:], start=True, stop=True)
            last.then_inc(base_mm, 1)
            pe.wait_ge(const_pool, CONST_POOL)
            pe.wait_ge(c_wq, 16)
            pe.wait_ge(c_wk, 16)
            stage_kq(0)
            stage_gate(0, 1, 11)
            pe.wait_ge(c_wv, 16)
            stage_v(0)
            pe.wait_ge(const_dve, 3)
            for c in range(NQ):
                scores(0, 0, 0, 0, c)
            max_rows(0)
            pe.wait_ge(c_wo, 16)

            def slot(g, par, t, a, now, nxt, old1, old2, old3):
                n = T * g + t
                gn, pn, tn = (g, par, t + 1) if t < T - 1 else (g + 1, 1 - par, 0)
                for c in range(NQ):
                    if nxt:
                        scores(n + 1, gn, pn, tn, c)
                    if now:
                        shifted(n, par, t, c)
                        if c:
                            values(n, t, c - 1, old1)
                    if c == 0 and old1:
                        pe.wait_ge(os_ok, n)
                        if old3:
                            pe.wait_ge(cum_read, n - 2)
                        elif old2:
                            pe.wait_ge(y_ok, n - 1)
                        if now:
                            pe.wait_ge(mT_sb, n + 1)
                        for k in range(NQ):
                            last = nc.tensor.transpose(u_bank[:, k * P:(k + 1) * P], oS[:, k, :], ident[:])
                        last.then_inc(nat_done, 1)
                    if c == 1 and old2:
                        pe.wait_ge(x2_ok, n - 1)
                        if old1:
                            pe.wait_ge(o_ok, n)
                        elif old3:
                            pe.wait_ge(cum_read, n - 2)
                        for k in range(KC):
                            last = nc.tensor.transpose(u_bank[:, k * P:(k + 1) * P], pay[t % 2][:, k * P:(k + 1) * P], ident[:])
                        last.then_inc(x2t_done, 1)
                    if c == 2 and old1:
                        pe.wait_ge(o_ok, n)
                        if old2:
                            pe.wait_ge(x2t_sb, n - 1)
                        for k in range(KC):
                            last = nc.tensor.transpose(u_bank[:, k * P:(k + 1) * P], o[:, k * P:(k + 1) * P], ident[:])
                        last.then_inc(ot_done, 1)
                    if c == 3 and old2:
                        pe.wait_ge(x2t_sb, n - 1)
                        if old1:
                            pe.wait_ge(ot_sb, n)
                        for k in range(KC):
                            last = nc.tensor.matmul(u_bank[:, 0:E], x2T[:, k, :], wr_sb[:, k, :],
                                                    start=k == 0, stop=k == KC - 1)
                        last.then_inc(lg_done, 1)
                if now:
                    values(n, t, NQ - 1, old1)
                if old2:
                    pe.wait_ge(lg_read, n - 1)
                elif old1:
                    pe.wait_ge(ot_sb, n)
                if nxt:
                    pe.wait_ge(mT_sb, n + 1)
                    max_rows(n + 1)
                if old1:
                    pe.wait_ge(ot_sb, n)
                    if nxt:
                        pe.wait_ge(mT_sb, n + 2)
                    for k in range(KC):
                        last = nc.tensor.matmul(u_bank[:, 0:D], oT[:, k, :], wo_sb[:, k, :], start=k == 0, stop=k == KC - 1)
                    last.then_inc(op_done, 1)
                if a and t == 0:
                    stage_kq(g + 1)
                if a and t == 1:
                    stage_gate(g + 1, 1, 11)
                if a and t == 3:
                    stage_v(g + 1)
                if old2:
                    pe.wait_ge(hot_ok, n - 1)
                    if old1:
                        pe.wait_ge(y_ok, n)
                    nc.tensor.matmul(u_bank[:, 0:E], before[:], hotb[:], start=True, stop=True)
                    nc.tensor.matmul(u_bank[:, E:2 * E], ones_b[:], hotb[:], start=True, stop=True).then_inc(cum_done, 1)

            for t in range(T):
                slot(0, 0, t, True, True, True, t >= 1, t >= 2, t >= 3)
            with pe.Fori(0, (G - 2) // 2) as gg:
                for par in (1, 0):
                    for t in range(T):
                        slot(2 * gg + 2 - par, par, t, True, True, True, True, True, True)
            for t in range(T):
                slot(G - 1, 1, t, False, True, t < T - 1, True, True, True)
            slot(G, 0, 0, False, False, False, True, True, True)
            slot(G, 0, 1, False, False, False, False, True, True)

            pe.wait_ge(cum_read, B)
            pe.wait_ge(w_exp, 32 * E)
            pe.wait_ge(table_ok, 1)

            def tile_x(j, i, jj, first):
                pe.wait_ge(f_in[i], 16 * (jj + 1))
                if not first:
                    pe.wait_ge(f_xts, j - 1)
                for k in range(KC):
                    last = nc.tensor.transpose(banks[i][:, k * P:(k + 1) * P], xf[i][:, k * P:(k + 1) * P], ident[:])
                last.then_inc(f_xt, 1)

            def tile_h(j, i, e, first):
                pe.wait_ge(f_xts, j + 1)
                if not first:
                    pe.wait_ge(f_hs, j - 1)
                for k in range(KC):
                    last = nc.tensor.matmul(banks[2 + i][:], xfT[i][:, k, :],
                                            w1_sb[:, bass.ds(e, 1), k, :].rearrange("p e f -> p (e f)"),
                                            start=k == 0, stop=k == KC - 1)
                last.then_inc(f_h, 1)

            def tile_ht(j, i, first):
                pe.wait_ge(f_hs, j + 1)
                if not first:
                    pe.wait_ge(f_hts, j - 1)
                for k in range(FC):
                    last = nc.tensor.transpose(banks[4 + i][:, k * P:(k + 1) * P], hs[i][:, k * P:(k + 1) * P], ident[:])
                last.then_inc(f_ht, 1)

            def tile_y(j, i, e, first):
                pe.wait_ge(f_hts, j + 1)
                if not first:
                    pe.wait_ge(f_ys, j - 1)
                for k in range(FC):
                    last = nc.tensor.matmul(banks[6 + i][:, 0:D], hT[i][:, k, :],
                                            w2_sb[:, bass.ds(e, 1), k, :].rearrange("p e f -> p (e f)"),
                                            start=k == 0, stop=k == FC - 1)
                last.then_inc(f_y, 1)

            def expert(j):
                return pe.value_load(tile_eu[0:1, bass.ds(j, 1)], min_val=0, max_val=E - 1)

            def pair(jj, first):
                j = 2 * jj
                tile_x(j, 0, jj, first)
                if not first:
                    tile_ht(j - 1, 1, False if not isinstance(jj, int) else jj < 2)
                tile_h(j, 0, expert(j), first)
                if not first:
                    tile_y(j - 1, 1, expert(j - 1), False if not isinstance(jj, int) else jj < 2)
                tile_x(j + 1, 1, jj, first)
                tile_ht(j, 0, first)
                tile_h(j + 1, 1, expert(j + 1), first)
                tile_y(j, 0, expert(j), first)

            pair(0, True)
            pair(1, False)
            with pe.Fori(2, TILES // 2) as jj:
                pair(jj, False)
            tile_ht(TILES - 1, 1, False)
            tile_y(TILES - 1, 1, expert(TILES - 1), False)


_INS = ["x", "ctxT", "mask", "maskT", "gx", "gf", "wqT", "wkT", "wvT", "woT", "wb1", "wb2T", "gate1", "gate2",
        "wr", "w1", "w2"]


def kernel(x, ctx_1024, mask_1x1xSxS2_bf1, g_xattn, g_ffn, L0_xattn_wq, L0_xattn_wk, L0_xattn_wv, L0_xattn_wo,
           L0_xattn_wb1, L0_xattn_wb2, L0_xattn_wg1, L0_xattn_wg2, L0_ffn_router_w, L0_ffn_w1, L0_ffn_w2):
    import numpy as np
    import concourse.bacc as bacc
    from concourse.bass_utils import run_bass_kernel_spmd

    mask = np.asarray(mask_1x1xSxS2_bf1)[0, 0].view(np.uint8)
    wg1, wg2 = np.asarray(L0_xattn_wg1), np.asarray(L0_xattn_wg2)
    gate1 = np.zeros((P, PAIRS, P), np.float32)
    gate2 = np.zeros((P, 2 * DH), np.float32)
    for a in range(2):
        for pair in range(PAIRS):
            row = 2 * DH * pair + DH * a
            gate1[row:row + DH, pair, HID * a:HID * (a + 1)] = wg1.T
        gate2[HID * a:HID * (a + 1), DH * a:DH * (a + 1)] = wg2.T
    arrays = {
        "x": np.asarray(x),
        "ctxT": np.asarray(ctx_1024).reshape(TOK, D).T,
        "mask": mask,
        "maskT": mask.T,
        "gx": np.asarray(g_xattn).reshape(1, 1),
        "gf": np.asarray(g_ffn).reshape(1, 1),
        "wqT": np.asarray(L0_xattn_wq).T,
        "wkT": np.asarray(L0_xattn_wk).T,
        "wvT": np.asarray(L0_xattn_wv).T,
        "woT": np.asarray(L0_xattn_wo).T,
        "wb1": np.asarray(L0_xattn_wb1),
        "wb2T": np.asarray(L0_xattn_wb2).T,
        "gate1": gate1,
        "gate2": gate2,
        "wr": np.asarray(L0_ffn_router_w),
        "w1": np.asarray(L0_ffn_w1),
        "w2": np.asarray(L0_ffn_w2),
    }
    nc = bacc.Bacc("TRN2", target_bir_lowering=False, num_devices=1)
    args = []
    for name in _INS:
        arrays[name] = np.ascontiguousarray(arrays[name])
        a = arrays[name]
        args.append(nc.dram_tensor(f"in_{name}", a.shape, mybir.dt.from_np(a.dtype), kind="ExternalInput").ap())
    args.append(nc.dram_tensor("out_0", (B, S, D), F32, kind="ExternalOutput").ap())
    build(nc, *args)
    got = run_bass_kernel_spmd(nc, [{f"in_{n}": arrays[n] for n in _INS}], core_ids=[0])
    return got.results[0]["out_0"]
```

```python
import math

import concourse.bass as bass
from concourse import mybir
from concourse.alu_op_type import AluOpType as ALU

F32 = mybir.dt.float32
BF16 = mybir.dt.bfloat16
U32 = mybir.dt.uint32
U8 = mybir.dt.uint8
ACT = mybir.ActivationFunctionType
AX = mybir.AxisListType

B, S, D = 32, 128, 256
H, DH = 16, 16
P = 128
T = 4
G = B // T
GT = T * S
KC = D // P
HC = H // KC
HID = 64
PAIRS = HC // 2
QH = 4
NQ = H // QH
TERMS_Q = (0, 0, 1, 0, 2, 1)
TERMS_K = (0, 1, 0, 2, 0, 1)
NT = len(TERMS_Q)
KR = NT * DH
MR = 3
VW = 32
TWO_ONES = 1.0 + 0x3f80 * 2.0 ** -23
NEG = -float(2.0 ** 100)
N_CONTEXT = 512
E, F = 8, 512
FC = F // P
TOK = B * S
REGION = TOK + P
TILES = 72
SPARE = TILES - 2 * TOK // P
TB = 4
RESULTS = TOK + TB * P
PW = D + 4
PAD_ROWS = E * REGION
A_USES = 20
EPS = 1e-5
SMALL = 9
CONST_POOL = 18
META_LINKS = 3
LINKS = 86


def build(nc, x, ctxT, mask, maskT, gx, gf, wqT, wkT, wvT, woT, wb1, wb2T, gate1, gate2, wr, w1, w2, out):
    from contextlib import ExitStack

    x_t = x.rearrange("b s d -> s b d")
    ctx_t = ctxT.rearrange("(c p) t -> p c t", p=P)
    out_t = out.rearrange("b s d -> s b d")

    ctx = ExitStack()
    with ctx:
        def sb(name, shape, dt=F32):
            return ctx.enter_context(nc.sbuf_tensor(name, shape, dt))

        def sem(name):
            return ctx.enter_context(nc.semaphore(name))

        kparts_d = nc.dram_tensor("kparts_d", [D, 3, GT], BF16, kind="Internal").ap()
        qparts_d = nc.dram_tensor("qparts_d", [D, 3, GT], BF16, kind="Internal").ap()
        rows_d = nc.dram_tensor("rows_d", [E * REGION + SPARE * P, PW], F32, kind="Internal").ap()
        ffn_d = nc.dram_tensor("ffn_d", [2 * RESULTS, D], F32, kind="Internal").ap()

        xy = sb("xy", [P, B, D])
        stack = sb("stack", [P, 2, 2, H, GT], BF16)
        w1_sb = stack[:, 0, :, :, :].rearrange("p a h t -> p (a h t)").bitcast(F32)\
            .rearrange("p (e c f) -> p e c f", e=E, c=KC)
        w2_sb = stack[:, 1, :, :, :].rearrange("p a h t -> p (a h t)").bitcast(F32)\
            .rearrange("p (e c f) -> p e c f", e=E, c=FC)
        ident = sb("ident", [P, P])
        identb = sb("identb", [P, P], BF16)
        ones_b = sb("ones_b", [P, P], BF16)
        before = sb("before", [P, P], BF16)
        mask_u = sb("mask_u", [P, 2, P], U8)
        bias_b = sb("bias_b", [P, 2, P], BF16)
        seen = sb("seen", [P, 4])
        gates = sb("gates", [P, 2])
        graw = sb("graw", [P, 2])
        wq_sb, wk_sb, wv_sb, wo_sb = (sb(n, [P, KC, D]) for n in ("wq_sb", "wk_sb", "wv_sb", "wo_sb"))
        g1_sb = sb("g1_sb", [P, PAIRS, P])
        g2_sb = sb("g2_sb", [P, 2 * DH])
        wr_sb = sb("wr_sb", [P, KC, E])
        wb1_sb = sb("wb1_sb", [HID, 1])
        wb1g = sb("wb1g", [HID, 1])
        wb2_sb = sb("wb2_sb", [HID, D])
        base = sb("base", [P, KC])
        ctxg = sb("ctxg", [P, KC, GT])
        xn = sb("xn", [P, T, D])
        xnT = sb("xnT", [P, KC, GT])
        qT = sb("qT", [P, KC, GT])
        kT = sb("kT", [P, KC, GT])
        th = sb("th", [P, KC, GT])
        hid = sb("hid", [P, PAIRS, GT])
        rest = sb("rest", [P, GT])
        krest = sb("krest", [P, GT])
        q3 = sb("q3", [P, KC, 3, GT], BF16)
        k3 = sb("k3", [P, KC, 3, GT], BF16)
        v = sb("v", [P, T, H, VW])
        pT = sb("pT", [P, NQ, QH * P])
        stats = sb("stats", [P, T, 6])
        mv = sb("mv", [P, T, 2])
        rstd = sb("rstd", [P, T])
        half = sb("half", [P, T])
        m_neg = sb("m_neg", [P, H])
        m_rest = sb("m_rest", [P, 2, H])
        m3 = sb("m3", [P, MR, H], BF16)
        m3T = sb("m3T", [MR * H, P], BF16)
        oS = sb("oS", [P, NQ, P])
        rden = sb("rden", [P, H])
        o = sb("o", [P, D])
        turned = sb("turned", [P, 2 * KC, P])
        stats2 = sb("stats2", [P, 6])
        mv2 = sb("mv2", [P, 2])
        rstd2 = sb("rstd2", [P, 1])
        pay = [sb(f"pay{i}", [P, PW]) for i in range(2)]
        dest = [sb(f"dest{i}", [P, 2], U32) for i in range(2)]
        logit = sb("logit", [P, E])
        top = sb("top", [P, E])
        topi = sb("topi", [P, E], U32)
        topf = sb("topf", [P, 2])
        r1 = sb("r1", [P, 4])
        hot = sb("hot", [P, 3, E])
        hotb = sb("hotb", [P, E], BF16)
        iota8 = sb("iota8", [P, E])
        region0 = sb("region0", [P, E])
        count = sb("count", [P, E])
        pos = sb("pos", [P, 3, E])
        destf = sb("destf", [P, 2])
        tokid = sb("tokid", [P, 1])
        rowf = sb("rowf", [P, 1])
        nrow = sb("nrow", [P, E, 32])
        thr = sb("thr", [P, E, 32])
        ntile = sb("ntile", [P, E])
        ends = sb("ends", [P, E])
        jump = sb("jump", [P, E])
        iotaj = sb("iotaj", [P, TILES])
        past = sb("past", [P, TILES, E])
        jumps = sb("jumps", [P, TILES, E])
        tile_e = sb("tile_e", [P, TILES])
        tile_r = sb("tile_r", [P, TILES])
        tile_eu = sb("tile_eu", [P, TILES], U32)
        tile_ru = sb("tile_ru", [P, TILES], U32)
        padf = sb("padf", [P, E])
        padi = [sb(f"padi{e}", [P, 1], U32) for e in range(E)]
        zrow = sb("zrow", [P, PW])
        xf = [(q3, k3)[i // 2][:, i % 2, :, :].rearrange("p a t -> p (a t)").bitcast(F32)[:, 0:PW] for i in range(TB)]
        xfT = [xnT[:, i, 0:D].rearrange("p (c t) -> p c t", c=KC) for i in range(2)]
        hT = [qT[:, i, :] for i in range(2)]
        w1t = [hid[:, KC * i:KC * (i + 1), :] for i in range(2)]
        ys = [th[:, i // 2, i % 2 * D:(i % 2 + 1) * D] for i in range(TB)]
        ymeta = [sb(f"ymeta{i}", [P, 6]) for i in range(TB)]
        ydest = [sb(f"ydest{i}", [P, 1], U32) for i in range(TB)]
        fin = [[hid[:, 2 * i + s, :] for s in range(2)] for i in range(2)]

        banks = [ctx.enter_context(nc.psum_tensor(f"bank{i}", [P, 512], F32)) for i in range(8)]
        sq_bank, sk_bank, a_bank, o_bank, u_bank = banks[0:2], banks[2:4], banks[4:6], banks[6], banks[7]
        mT_ps = u_bank[0:MR * H, 0:P // 2].bitcast(BF16)

        c_wq, c_wk, c_wv, c_wo = sem("wq_loaded"), sem("wk_loaded"), sem("wv_loaded"), sem("wo_loaded")
        c_small = sem("small_loaded")
        c_x0, c_x = sem("x_first_loaded"), sem("x_rest_loaded")
        ctx_in = sem("ctx_loaded")
        w1_in, w2_in = sem("w1_loaded"), sem("w2_loaded")
        const_pool, const_dve = sem("pool_constants"), sem("dve_constants")
        gelu_b, base_mm, base_ok = sem("wb1_gelu"), sem("base_product"), sem("base_ready")
        gates_ok = sem("gates_ready")
        ln_var, ln_rstd, xn_ok = sem("ln_variance"), sem("ln_rstd"), sem("xn_ready")
        a_done, a_free = sem("projection_done"), sem("projection_read")
        q3_ok, k3_ok = sem("q_parts_ready"), sem("k_parts_ready")
        qb, kb = sem("q_parts_stored"), sem("k_parts_stored")
        q_st = [sem("q_stack_low_heads"), sem("q_stack_high_heads")]
        k_st, k3_high = sem("k_stack_loaded"), sem("k_high_parts")
        s_done, max_done = sem("scores_done"), sem("max_done")
        m3_ok, mT_sb, m_in = sem("max_parts"), sem("max_copied"), sem("max_rows_loaded")
        st_done, exp_done, pv_done = sem("shifted_scores_done"), sem("exp_done"), sem("pv_done")
        os_ok, nat_done, o_ok = sem("strips_copied"), sem("strips_transposed"), sem("o_ready")
        turn_done, turn_sb = sem("turned_done"), sem("turned_ready")
        lo_done, lo_read = sem("output_and_logits_done"), sem("output_and_logits_read")
        m_done = sem("max_turned")
        c_done, c_read = sem("counts_done"), sem("counts_read")
        l2_var, l2_rstd, x2_ok = sem("ln2_variance"), sem("ln2_rstd"), sem("x2_ready")
        gap_ok, gap_exp = sem("gap_ready"), sem("gap_exp")
        hot_ok = sem("hot_ready")
        dest_ok = sem("dest_ready")
        sc = [sem("rows_sent_even"), sem("rows_sent_odd")]
        pad_ok, pad_in = sem("padding_index"), sem("padding_sent")
        table_ok = sem("tile_table")
        sp_passed, pool_passed, dve_passed, pe_passed = (sem(n) for n in ("sp_passed", "pool_passed", "dve_passed", "pe_passed"))
        dch, ach, pch = sem("dve_chain"), sem("act_chain"), sem("pool_chain")
        f_in = [sem(f"tile_loaded_{i}") for i in range(TB)]
        f_xt, f_xts = sem("tile_transposed"), sem("tile_xT_ready")
        f_h, f_hs = sem("hidden_done"), sem("hidden_silu")
        f_w1 = sem("w1_of_tile")
        f_y, f_ys = sem("tile_product"), sem("tile_scaled")
        f_out = [sem(f"tile_sent_{i}") for i in range(TB)]
        e_in = [sem("result_parts_even"), sem("result_parts_odd")]
        e_add = sem("result_added")
        e_out = sem("result_stored")

        block = ctx.enter_context(nc.Block())

        def head(par, side, h, t, rows):
            return stack[0:rows, par, side, h, t * P:(t + 1) * P]

        @block.sync
        def _(sp):
            sp.dma_start(xy[:, 0:T, :], x_t[:, 0:T, :]).then_inc(c_x0, 16)
            sp.dma_start(ctxg[:], ctx_t[:, :, 0:GT]).then_inc(ctx_in, 16)
            for w_sb, w, c in ((wq_sb, wqT, c_wq), (wk_sb, wkT, c_wk)):
                sp.dma_start(w_sb[:], w.rearrange("(c p) n -> p c n", p=P)).then_inc(c, 16)
            small = (
                (wb1_sb[:], wb1), (wb2_sb[:], wb2T), (g1_sb[:], gate1), (g2_sb[:], gate2),
                (mask_u[:, 0, :], mask), (mask_u[:, 1, :], maskT),
                (graw[:, 0:1], gx.broadcast_to([P, 1])), (graw[:, 1:2], gf.broadcast_to([P, 1])),
                (wr_sb[:], wr.rearrange("(c p) e -> p c e", p=P)),
            )
            assert len(small) == SMALL
            for to, of in small:
                sp.dma_start(to, of).then_inc(c_small, 16)
            for w_sb, w, c in ((wv_sb, wvT, c_wv), (wo_sb, woT, c_wo)):
                sp.dma_start(w_sb[:], w.rearrange("(c p) n -> p c n", p=P)).then_inc(c, 16)
            sp.dma_start(xy[:, T:B, :], x_t[:, T:B, :]).then_inc(c_x, 16)

            def store_k(g, first):
                sp.wait_ge(k3_ok, g + 1)
                sp.sem_inc(sp_passed, 1)
                if not first:
                    sp.wait_ge(k_st, 16 * NT * g)
                sp.dma_start(kparts_d.rearrange("(c p) s t -> p c s t", p=P), k3[:]).then_inc(kb, 16)

            def load_k(g, par):
                sp.wait_ge(kb, 16 * (g + 1))
                for j, part in enumerate(TERMS_K):
                    sp.dma_start(stack[DH * j:DH * (j + 1), par, 1, :, :],
                                 kparts_d[:, part, :].rearrange("(h d) t -> d h t", d=DH)).then_inc(k_st, 16)

            def store_q(g, c, first):
                sp.wait_ge(q3_ok, KC * g + c + 1)
                sp.sem_inc(sp_passed, 1)
                if not first:
                    sp.wait_ge(q_st[c], 16 * NT * g)
                sp.dma_start(qparts_d[c * P:(c + 1) * P, :, :], q3[:, c, :, :]).then_inc(qb, 16)

            def load_q(g, c, par):
                sp.wait_ge(qb, 16 * (KC * g + c + 1))
                for j, part in enumerate(TERMS_Q):
                    sp.dma_start(stack[DH * j:DH * (j + 1), par, 0, HC * c:HC * (c + 1), :],
                                 qparts_d[c * P:(c + 1) * P, part, :].rearrange("(h d) t -> d h t", d=DH))\
                        .then_inc(q_st[c], 16)

            def load_max(n, par, t):
                sp.wait_ge(mT_sb, n + 1)
                sp.dma_start(stack[KR:KR + MR, par, 0, :, t * P:(t + 1) * P],
                             m3T[:, :]).then_inc(m_in, 16)

            store_k(0, True)
            load_k(0, 0)
            for c in range(KC):
                store_q(0, c, True)
                load_q(0, c, 0)
            load_max(0, 0, 0)

            def group(g, par, last):
                n = T * g
                if not last:
                    sp.wait_ge(a_done, A_USES * (g + 1))
                    sp.dma_start(ctxg[:], ctx_t[:, :, bass.ds((g + 1) * GT, GT)]).then_inc(ctx_in, 16)
                load_max(n + 1, par, 1)
                if not last:
                    store_k(g + 1, False)
                    store_q(g + 1, 0, False)
                    load_k(g + 1, 1 - par)
                load_max(n + 2, par, 2)
                if not last:
                    load_q(g + 1, 0, 1 - par)
                    store_q(g + 1, 1, False)
                    load_q(g + 1, 1, 1 - par)
                if last:
                    load_w2(0)
                load_max(n + 3, par, 3)
                if last:
                    load_w2(1)
                else:
                    load_max(n + 4, 1 - par, 0)

            def load_w2(t):
                sp.wait_ge(st_done, NQ * (T * (G - 1) + t + 1))
                cols = slice(D // T * t, D // T * (t + 1))
                for e in range(E):
                    sp.dma_start(w2_sb[:, e, :, cols], w2[e, :, cols].rearrange("(c p) f -> p c f", p=P)).then_inc(w2_in, 16)

            group(0, 0, False)
            with sp.Fori(0, (G - 2) // 2) as gg:
                group(2 * gg + 1, 1, False)
                group(2 * gg + 2, 0, False)
            group(G - 1, 1, True)
            load_w2(2)
            load_w2(3)

            sp.wait_ge(table_ok, 1)
            sp.wait_ge(sc[0], 32 * B // 2)
            sp.wait_ge(sc[1], 32 * B // 2)
            sp.wait_ge(pad_in, 16 * (E + SPARE))

            def load_tile(j, i, first):
                row = sp.value_load(tile_ru[0:1, bass.ds(j, 1)], min_val=0, max_val=E * REGION + (SPARE - 1) * P)
                if not first:
                    sp.wait_ge(f_ys, j - TB + 1)
                sp.dma_start(xf[i], rows_d[bass.ds(row, P), :]).then_inc(f_in[i], 16)

            for i in range(TB):
                load_tile(i, i, True)
            with sp.Fori(1, TILES // TB) as jj:
                for i in range(TB):
                    load_tile(TB * jj + i, i, False)

            for sent in f_out:
                sp.wait_ge(sent, 16 * TILES // TB)

            def load_result(k, i, first):
                if not first:
                    sp.wait_ge(e_add, k - 1)
                    sp.sem_inc(sp_passed, 1)
                for s in range(2):
                    sp.dma_start(fin[i][s].rearrange("p (u d) -> p u d", d=D),
                                 ffn_d[bass.ds(s * RESULTS + k * 2 * P, 2 * P), :].rearrange("(u p) d -> p u d", p=P))\
                        .then_inc(e_in[i], 16)

            def store_result(k):
                sp.wait_ge(e_add, k + 1)
                sp.sem_inc(sp_passed, 1)
                sp.dma_start(out_t[:, bass.ds(2 * k, 2), :], xy[:, bass.ds(2 * k, 2), :]).then_inc(e_out, 16)

            load_result(0, 0, True)
            load_result(1, 1, True)
            with sp.Fori(1, B // 4) as kk:
                store_result(2 * kk - 2)
                load_result(2 * kk, 0, False)
                store_result(2 * kk - 1)
                load_result(2 * kk + 1, 1, False)
            store_result(B // 2 - 2)
            store_result(B // 2 - 1)
            sp.wait_ge(e_out, 16 * (B // 2))

        @block.gpsimd
        def _(pool):
            nc.gpsimd.memset(ident[:], 0.0).then_inc(const_pool, 1)
            nc.gpsimd.memset(identb[:], 0.0).then_inc(const_pool, 1)
            nc.gpsimd.memset(before[:], 1.0).then_inc(const_pool, 1)
            pool.wait_ge(const_pool, 3)
            for m in (ident, identb):
                nc.gpsimd.affine_select(out=m[:], in_=m[:], compare_op=ALU.not_equal, fill=1.0, base=0,
                                        pattern=[[-1, P]], channel_multiplier=1).then_inc(const_pool, 1)
            nc.gpsimd.affine_select(out=before[:], in_=before[:], compare_op=ALU.is_gt, fill=0.0, base=0,
                                    pattern=[[1, P]], channel_multiplier=-1).then_inc(const_pool, 1)
            nc.gpsimd.memset(half[:], -0.5).then_inc(const_pool, 1)
            nc.gpsimd.memset(v[:], 0.0).then_inc(const_pool, 1)
            pool.wait_ge(const_pool, 8)
            nc.gpsimd.memset(v[:, :, :, DH:DH + 1], 1.0).then_inc(const_pool, 1)
            nc.gpsimd.iota(iota8[:], pattern=[[1, E]], base=0, channel_multiplier=0,
                           allow_small_or_imprecise_dtypes=True).then_inc(const_pool, 1)
            nc.gpsimd.iota(region0[:], pattern=[[REGION, E]], base=0, channel_multiplier=0,
                           allow_small_or_imprecise_dtypes=True).then_inc(const_pool, 1)
            nc.gpsimd.iota(tokid[:], pattern=[[0, 1]], base=0, channel_multiplier=1,
                           allow_small_or_imprecise_dtypes=True).then_inc(const_pool, 1)
            nc.gpsimd.iota(thr[:], pattern=[[0, E], [P, 32]], base=0, channel_multiplier=0,
                           allow_small_or_imprecise_dtypes=True).then_inc(const_pool, 1)
            nc.gpsimd.iota(iotaj[:], pattern=[[1, TILES]], base=0, channel_multiplier=0,
                           allow_small_or_imprecise_dtypes=True).then_inc(const_pool, 1)
            nc.gpsimd.memset(zrow[:], 0.0).then_inc(const_pool, 1)
            nc.gpsimd.memset(count[:], 0.0).then_inc(const_pool, 1)
            nc.gpsimd.iota(rowf[:], pattern=[[0, 1]], base=0, channel_multiplier=1,
                           allow_small_or_imprecise_dtypes=True).then_inc(const_pool, 1)
            pool.wait_ge(const_pool, CONST_POOL - 1)
            nc.gpsimd.iota(zrow[:, PW - 1:PW], pattern=[[0, 1]], base=TOK, channel_multiplier=1,
                           allow_small_or_imprecise_dtypes=True).then_inc(const_pool, 1)
            pool.wait_ge(const_pool, CONST_POOL)
            for i in range(SPARE):
                pool.dma_start(rows_d[PAD_ROWS + i * P:PAD_ROWS + (i + 1) * P, :], zrow[:]).then_inc(pad_in, 16)

            def rstd_of(g):
                pool.wait_ge(ln_var, g + 1)
                nc.gpsimd.tensor_tensor(rstd[:], mv[:, :, 1], half[:], ALU.pow).then_inc(ln_rstd, 1)

            def split_k(g, first):
                pool.wait_ge(k3_high, g + 1)
                pool.sem_inc(pool_passed, 1)
                pool.wait_ge(a_free, A_USES * g + KC)
                for c in range(KC):
                    w = (3 * KC - 1) * g + 3 * c
                    nc.gpsimd.tensor_tensor(krest[:], kT[:, c, :], k3[:, c, 0, :], ALU.subtract).then_inc(pch, 1)
                    pool.wait_ge(pch, w + 1)
                    pool.sem_inc(pool_passed, 1)
                    nc.gpsimd.tensor_copy(k3[:, c, 1, :], krest[:]).then_inc(pch, 1)
                    pool.wait_ge(pch, w + 2)
                    last = nc.gpsimd.tensor_tensor(k3[:, c, 2, :], krest[:], k3[:, c, 1, :], ALU.subtract)
                    if c < KC - 1:
                        last.then_inc(pch, 1)
                        pool.wait_ge(pch, w + 3)
                last.then_inc(k3_ok, 1)

            def rstd2_of(r):
                pool.wait_ge(l2_var, r + 1)
                nc.gpsimd.tensor_tensor(rstd2[:], mv2[:, 1:2], half[:, 0:1], ALU.pow).then_inc(l2_rstd, 1)

            def send(r, i):
                pool.wait_ge(dest_ok, r + 1)
                pool.sem_inc(pool_passed, 1)
                for s in range(2):
                    pool.indirect_dma_start(rows_d, bass.IndirectOffsetOnAxis(ap=dest[i][:, s:s + 1], axis=0),
                                            pay[i][:], None).then_inc(sc[i], 16)

            rstd_of(0)
            split_k(0, True)

            def slot(g, t, a, old1, old3):
                n = T * g + t
                if a and t == 0:
                    rstd_of(g + 1)
                if old3:
                    send(n - 3, (t + 1) % 2)
                if old1:
                    rstd2_of(n - 1)
                if a and t == 0:
                    split_k(g + 1, False)

            for t in range(T):
                slot(0, t, True, t >= 1, t >= 3)
            with pool.Fori(1, G - 1) as g:
                for t in range(T):
                    slot(g, t, True, True, True)
            for t in range(T):
                slot(G - 1, t, False, True, True)
            slot(G, 0, False, True, True)
            slot(G, 1, False, False, True)
            slot(G, 2, False, False, True)
            pool.wait_ge(pad_ok, 1)
            for e in range(E):
                pool.indirect_dma_start(rows_d, bass.IndirectOffsetOnAxis(ap=padi[e][:, 0:1], axis=0),
                                        zrow[:], None).then_inc(pad_in, 16)

            def send_tile(j, i):
                pool.wait_ge(f_ys, j + 1)
                pool.sem_inc(pool_passed, 1)
                pool.indirect_dma_start(ffn_d, bass.IndirectOffsetOnAxis(ap=ydest[i][:, 0:1], axis=0),
                                        ys[i], None).then_inc(f_out[i], 16)

            with pool.Fori(0, TILES // TB) as jj:
                for i in range(TB):
                    send_tile(TB * jj + i, i)

        @block.scalar
        def _(act):
            act.wait_ge(c_small, 16 * SMALL)
            nc.scalar.activation(wb1g[:], wb1_sb[:], ACT.Gelu, scale=math.log(N_CONTEXT)).then_inc(gelu_b, 1)
            nc.scalar.activation(gates[:], graw[:], ACT.Tanh).then_inc(gates_ok, 1)

            def evac(g, u, to, func=None):
                act.wait_ge(a_done, A_USES * g + u + 1)
                nc.scalar.activation(to, a_bank[u % 2][:, 0:to_width(to)], func or ACT.Copy).then_inc(a_free, 1)

            def to_width(to):
                return math.prod(to.shape[1:])

            def stage_k(g, first):
                if not first:
                    act.wait_ge(k3_ok, g)
                    act.wait_ge(kb, 16 * g)
                for c in range(KC):
                    act.wait_ge(a_done, A_USES * g + c + 1)
                    last = nc.scalar.activation(k3[:, c, 0, :], a_bank[c][:], ACT.Copy)
                    if c == KC - 1:
                        last.then_inc(k3_high, 1)
                    evac(g, c, kT[:, c, :])

            def stage_q(g, first):
                for c in range(KC):
                    evac(g, 2 + c, xnT[:, c, :])
                if not first:
                    act.wait_ge(q3_ok, KC * g)
                for c in range(KC):
                    evac(g, 4 + c, qT[:, c, :])

            def hidden(g, u):
                for p in range(PAIRS):
                    evac(g, u + p, hid[:, p, :], ACT.Gelu)

            def gate(g, c, u):
                evac(g, u + PAIRS, th[:, c, :], ACT.Tanh)

            def stage_v(g, ts=range(T)):
                for t in ts:
                    act.wait_ge(a_done, A_USES * g + 16 + t + 1)
                    nc.scalar.activation(v[:, t, :, 0:DH],
                                         a_bank[t % 2][:, 0:D].rearrange("p (h d) -> p h d", d=DH),
                                         ACT.Copy).then_inc(a_free, 1)

            stage_k(0, True)
            stage_q(0, True)
            for c, u in ((0, 6), (1, 11)):
                hidden(0, u)
                gate(0, c, u)
            act.wait_ge(const_pool, CONST_POOL)
            stage_v(0)

            def slot(g, t, a, now, old1, old2):
                n = T * g + t
                if old1:
                    act.wait_ge(pv_done, NQ * n)
                    if old2:
                        act.wait_ge(nat_done, n - 1)
                    nc.scalar.activation(oS[:].rearrange("p c q -> p (c q)"), o_bank[:], ACT.Copy).then_inc(os_ok, 1)
                for c in range(NQ):
                    if now:
                        act.wait_ge(st_done, NQ * n + c + 1)
                        if old1:
                            act.wait_ge(pv_done, NQ * (n - 1) + c + 1)
                        nc.scalar.activation(pT[:, c, :], sk_bank[c % 2][:], ACT.Exp).then_inc(exp_done, 1)
                    if c == 1 and (old1 or old2):
                        a0, a1 = 0 if old1 else KC, 2 * KC if old2 else KC
                        act.wait_ge(turn_done, n)
                        nc.scalar.activation(turned[:, a0:a1, :].rearrange("p c t -> p (c t)"),
                                             u_bank[:, a0 * P:a1 * P], ACT.Copy).then_inc(turn_sb, 1)
                if a and t == 0:
                    stage_k(g + 1, False)
                    stage_q(g + 1, False)
                    hidden(g + 1, 6)
                if a and t == 1:
                    hidden(g + 1, 11)
                if a and t == 2:
                    stage_v(g + 1, (0,))
                if a and t == 3:
                    stage_v(g + 1, (2,))
                if old2:
                    act.wait_ge(gap_ok, n - 1)
                    nc.scalar.activation(r1[:, 1:2], r1[:, 0:1], ACT.Exp).then_inc(gap_exp, 1)
                if a and t == 0:
                    gate(g + 1, 0, 6)
                if a and t == 1:
                    gate(g + 1, 1, 11)
                if a and t == 2:
                    stage_v(g + 1, (1,))
                if a and t == 3:
                    stage_v(g + 1, (3,))

            for t in range(T):
                slot(0, t, True, True, t >= 1, t >= 2)
            with act.Fori(1, G - 1) as g:
                for t in range(T):
                    slot(g, t, True, True, True, True)
            act.wait_ge(st_done, NQ * T * (G - 1))
            for e in range(E):
                act.dma_start(w1_sb[:, e, :, :], w1[e, :, :].rearrange("(c p) f -> p c f", p=P)).then_inc(w1_in, 16)
            for t in range(T):
                slot(G - 1, t, False, True, True, True)
            slot(G, 0, False, False, True, True)
            slot(G, 1, False, False, False, True)

            def tile_x(j, i):
                act.wait_ge(f_xt, j + 1)
                nc.scalar.activation(xfT[i].rearrange("p c t -> p (c t)"), banks[i][:, 0:D], ACT.Copy).then_inc(f_xts, 1)

            def tile_h(j, i):
                act.wait_ge(f_h, j + 1)
                nc.scalar.activation(hT[i], banks[2 + i][:], ACT.Silu).then_inc(f_hs, 1)

            def tiles(jj, last):
                for i in range(TB):
                    j = TB * jj + i
                    if not last or i < TB - 2:
                        tile_x(j + 2, i % 2)
                    if not last or i < TB - 1:
                        tile_h(j + 1, (i + 1) % 2)

            tile_x(0, 0)
            tile_x(1, 1)
            tile_h(0, 0)
            with act.Fori(0, TILES // TB - 1) as jj:
                tiles(jj, False)
            tiles(TILES // TB - 1, True)

        @block.vector
        def _(dve):
            chain = [0, 0]

            def link(ins):
                chain[0] += 1
                ins.then_inc(dch, 1)
                dve.wait_ge(dch, chain[1] + chain[0])


            def layer_norm_stats(g):
                for t in range(T):
                    link(nc.vector.bn_stats(stats[:, t, :], xy[:, T * g + t, :]))
                for t in range(T):
                    dve.sem_inc(dve_passed, 1)
                    link(nc.vector.bn_aggr(mv[:, t, :], stats[:, t, :]))
                nc.vector.tensor_scalar(mv[:, :, 1], mv[:, :, 1], EPS, None, ALU.add).then_inc(ln_var, 1)

            def layer_norm(g, first):
                dve.wait_ge(ln_rstd, g + 1)
                if not first:
                    dve.wait_ge(a_done, A_USES * (g - 1) + 4)
                for t in range(T):
                    ins = nc.vector.tensor_scalar(xn[:, t, :], xy[:, T * g + t, :], mv[:, t, 0:1], rstd[:, t:t + 1],
                                                  ALU.subtract, ALU.mult)
                ins.then_inc(xn_ok, 1)

            def q_parts(g, c, first):
                dve.wait_ge(a_free, A_USES * g + (11 if c == 0 else 16))
                if not first:
                    dve.wait_ge(qb, 16 * (KC * g - (KC - 1 - c)))
                link(nc.vector.tensor_scalar(rest[:], qT[:, c, :], base[:, c:c + 1], None, ALU.mult))
                link(nc.vector.scalar_tensor_tensor(qT[:, c, :], th[:, c, :], 1.0, rest[:], ALU.add, ALU.mult))
                link(nc.vector.tensor_copy(q3[:, c, 0, :], qT[:, c, :]))
                link(nc.vector.tensor_tensor(rest[:], qT[:, c, :], q3[:, c, 0, :], ALU.subtract))
                link(nc.vector.tensor_copy(q3[:, c, 1, :], rest[:]))
                ins = nc.vector.tensor_tensor(q3[:, c, 2, :], rest[:], q3[:, c, 1, :], ALU.subtract)
                ins.then_inc(q3_ok, 1)
                if c == 0:
                    dve.wait_ge(q3_ok, KC * g + 1)

            def row_max(n, c):
                dve.wait_ge(s_done, NQ * n + c + 1)
                nc.vector.tensor_reduce(m_neg[:, QH * c:QH * (c + 1)],
                                        sq_bank[c % 2][:].rearrange("p (h k) -> p h k", h=QH),
                                        axis=AX.X, op=ALU.max, negate=True).then_inc(max_done, 1)

            def max_parts(n, first):
                dve.wait_ge(max_done, NQ * (n + 1))
                if not first:
                    dve.wait_ge(m_done, n)
                link(nc.vector.tensor_copy(m3[:, 0, :], m_neg[:]))
                link(nc.vector.tensor_tensor(m_rest[:, 0, :], m_neg[:], m3[:, 0, :], ALU.subtract))
                link(nc.vector.tensor_copy(m3[:, 1, :], m_rest[:, 0, :]))
                nc.vector.tensor_tensor(m3[:, 2, :], m_rest[:, 0, :], m3[:, 1, :], ALU.subtract).then_inc(m3_ok, 1)

            def copy_max(n, first):
                dve.wait_ge(m_done, n + 1)
                if not first:
                    dve.wait_ge(m_in, 16 * n)
                nc.vector.tensor_copy(m3T[:], mT_ps).then_inc(mT_sb, 1)

            dve.wait_ge(c_x0, 16)
            layer_norm_stats(0)
            layer_norm(0, True)
            dve.wait_ge(c_small, 16 * SMALL)
            link(nc.vector.tensor_scalar(bias_b[:], mask_u[:], -NEG, NEG, ALU.mult, ALU.add))
            link(nc.vector.tensor_reduce(seen[:, 0:1], mask_u[:, 0, :], axis=AX.X, op=ALU.max))
            link(nc.vector.reciprocal(seen[:, 1:2], seen[:, 0:1]))
            link(nc.vector.tensor_tensor(seen[:, 2:3], seen[:, 0:1], seen[:, 1:2], ALU.mult))
            dve.wait_ge(gates_ok, 1)
            nc.vector.tensor_tensor(seen[:, 3:4], seen[:, 2:3], gates[:, 0:1], ALU.mult).then_inc(const_dve, 1)
            dve.wait_ge(base_mm, 1)
            link(nc.vector.tensor_scalar(base[:], o_bank[:, 0:KC], DH ** -0.5, None, ALU.mult))
            q_parts(0, 0, True)
            q_parts(0, 1, True)
            nc.vector.memset(ones_b[:], 1.0).then_inc(const_dve, 1)
            nc.vector.memset(stack[KR:KR + MR, :, 1, :, :].bitcast(F32), TWO_ONES).then_inc(const_dve, 1)
            for c in range(NQ):
                row_max(0, c)
            max_parts(0, True)
            copy_max(0, True)
            row_max(1, 0)
            dve.wait_ge(mT_sb, 1)

            dve.wait_ge(const_pool, CONST_POOL)
            dve.wait_ge(const_dve, 3)

            def slot(g, t, a, nxt, nxt2, old1, old2, old3, reused):
                n = T * g + t
                for c in range(NQ):
                    if nxt and c < NQ - 1:
                        row_max(n + 1, c + 1)
                    if c == 1 and old3:
                        weights_and_rows(n - 3, (t + 1) % 2)
                    if c == 0 and old2:
                        normalise2(n - 2, t % 2, 2 * g + t // 2 - 1, reused)
                    if c == 0 and old1:
                        dve.wait_ge(nat_done, n)
                        if old2:
                            dve.wait_ge(turn_done, n - 1)
                        strips = u_bank[:].rearrange("p (h w) -> p h w", w=VW)
                        link(nc.vector.reciprocal(rden[:], strips[:, :, DH]))
                        nc.vector.tensor_tensor(o[:].rearrange("p (h d) -> p h d", d=DH), strips[:, :, 0:DH],
                                                rden[:].unsqueeze(2).to_broadcast([P, H, DH]), ALU.mult).then_inc(o_ok, 1)
                    if c == 0 and a and t == 0:
                        layer_norm_stats(g + 1)
                    if c == 1 and a and t == 0:
                        layer_norm(g + 1, False)
                    if c == 1 and a and t == 1:
                        q_parts(g + 1, 0, False)
                    if c == 0 and a and t == 2:
                        q_parts(g + 1, 1, False)
                if nxt:
                    max_parts(n + 1, False)
                if old1 or old2:
                    dve.wait_ge(lo_done, n)
                    if old1:
                        last = nc.vector.scalar_tensor_tensor(xy[:, n - 1, :], u_bank[:, 0:D], seen[:, 3:4],
                                                              xy[:, n - 1, :], ALU.mult, ALU.add)
                    if old2:
                        last = nc.vector.tensor_copy(logit[:], u_bank[:, D:D + E])
                    last.then_inc(lo_read, 1)
                    dve.wait_ge(lo_read, n)
                if nxt:
                    copy_max(n + 1, False)
                if old2:
                    experts_of(n - 2)
                if nxt2:
                    row_max(n + 2, 0)
                if old2:
                    dve.wait_ge(c_done, n - 1)
                    link(nc.vector.tensor_tensor(pos[:, 0, :], u_bank[:, D:D + E], count[:], ALU.add))
                    nc.vector.tensor_tensor(count[:], u_bank[:, D + E:D + 2 * E], count[:], ALU.add).then_inc(c_read, 1)
                if old1:
                    link(nc.vector.bn_stats(stats2[:], xy[:, n - 1, :]))
                    dve.sem_inc(dve_passed, 1)
                    link(nc.vector.bn_aggr(mv2[:], stats2[:]))
                    nc.vector.tensor_scalar(mv2[:, 1:2], mv2[:, 1:2], EPS, None, ALU.add).then_inc(l2_var, 1)

            def normalise2(r, i, kth, reused):
                dve.wait_ge(l2_rstd, r + 1)
                if reused:
                    dve.wait_ge(sc[i], 32 * kth)
                nc.vector.tensor_scalar(pay[i][:, 0:D], xy[:, r, :], mv2[:, 0:1], rstd2[:, 0:1],
                                        ALU.subtract, ALU.mult).then_inc(x2_ok, 1)

            def experts_of(r):
                dve.sem_inc(dve_passed, 1)
                link(nc.vector.max(top[:], logit[:]))
                nc.vector.tensor_tensor(r1[:, 0:1], top[:, 1:2], top[:, 0:1], ALU.subtract).then_inc(gap_ok, 1)
                link(nc.vector.max_index(topi[:], top[:], logit[:]))
                link(nc.vector.tensor_copy(topf[:], topi[:, 0:2]))
                for s in range(2):
                    ins = nc.vector.tensor_scalar(hot[:, s, :], iota8[:], topf[:, s:s + 1], None, ALU.is_equal)
                link(ins)
                nc.vector.tensor_tensor(hotb[:], hot[:, 0, :], hot[:, 1, :], ALU.add).then_inc(hot_ok, 1)

            def weights_and_rows(r, i):
                dve.wait_ge(c_read, r + 1)
                link(nc.vector.tensor_tensor(pos[:, 0, :], pos[:, 0, :], region0[:], ALU.add))
                for s in range(2):
                    ins = nc.vector.tensor_tensor(pos[:, 1 + s, :], pos[:, 0, :], hot[:, s, :], ALU.mult)
                link(ins)
                link(nc.vector.tensor_reduce(destf[:], pos[:, 1:3, :], axis=AX.X, op=ALU.add))
                nc.vector.tensor_copy(dest[i][:], destf[:])
                dve.wait_ge(gap_exp, r + 1)
                link(nc.vector.tensor_scalar(r1[:, 2:3], r1[:, 1:2], 1.0, None, ALU.add))
                link(nc.vector.reciprocal(r1[:, 3:4], r1[:, 2:3]))
                link(nc.vector.tensor_scalar(pay[i][:, D:D + 1], r1[:, 3:4], gates[:, 1:2], None, ALU.mult))
                nc.vector.tensor_tensor(pay[i][:, D + 1:D + 2], pay[i][:, D:D + 1], r1[:, 1:2], ALU.mult)
                nc.vector.tensor_copy(pay[i][:, D + 2:D + 3], topf[:, 0:1])
                nc.vector.tensor_copy(pay[i][:, D + 3:D + 4], tokid[:])
                nc.vector.tensor_scalar(tokid[:], tokid[:], float(S), None, ALU.add).then_inc(dest_ok, 1)
                dve.wait_ge(dest_ok, r + 1)

            for t in range(T):
                slot(0, t, True, True, True, t >= 1, t >= 2, t >= 3, False)
            first_links = chain[0]
            with dve.Fori(1, G - 1) as g:
                chain[:] = [0, first_links + (g - 1) * LINKS]
                for t in range(T):
                    slot(g, t, True, True, True, True, True, True, True)
                assert chain[0] == LINKS, chain[0]
            chain[:] = [0, first_links + (G - 2) * LINKS]
            for t in range(T):
                slot(G - 1, t, False, t < T - 1, t < T - 2, True, True, True, True)
            slot(G, 0, False, False, False, True, True, True, True)
            slot(G, 1, False, False, False, False, True, True, True)
            slot(G, 2, False, False, False, False, False, True, True)

            link(nc.vector.tensor_tensor(padf[:], count[:], region0[:], ALU.add))
            link(nc.vector.tensor_scalar(padf[:], padf[:], rowf[:, 0:1], None, ALU.add))
            for e in range(E):
                ins = nc.vector.tensor_copy(padi[e][:], padf[:, e:e + 1])
            ins.then_inc(pad_ok, 1)
            link(nc.vector.tensor_tensor(nrow[:], count[:].unsqueeze(2).to_broadcast([P, E, 32]), thr[:], ALU.is_gt))
            link(nc.vector.tensor_reduce(ntile[:], nrow[:], axis=AX.X, op=ALU.add))
            link(nc.vector.tensor_copy(ends[:, 0:1], ntile[:, 0:1]))
            for e in range(1, E):
                link(nc.vector.tensor_tensor(ends[:, e:e + 1], ends[:, e - 1:e], ntile[:, e:e + 1], ALU.add))
            link(nc.vector.tensor_scalar(jump[:], ntile[:], -float(P), float(REGION), ALU.mult, ALU.add))
            link(nc.vector.tensor_tensor(past[:], iotaj[:].unsqueeze(2).to_broadcast([P, TILES, E]),
                                         ends[:].unsqueeze(1).to_broadcast([P, TILES, E]), ALU.is_ge))
            link(nc.vector.tensor_tensor(jumps[:], past[:], jump[:].unsqueeze(1).to_broadcast([P, TILES, E]), ALU.mult))
            link(nc.vector.tensor_reduce(tile_e[:], past[:], axis=AX.X, op=ALU.add))
            link(nc.vector.tensor_scalar(tile_e[:], tile_e[:], float(E - 1), None, ALU.min))
            link(nc.vector.tensor_reduce(tile_r[:], jumps[:], axis=AX.X, op=ALU.add))
            link(nc.vector.scalar_tensor_tensor(tile_r[:], iotaj[:], float(P), tile_r[:], ALU.mult, ALU.add))
            link(nc.vector.tensor_copy(tile_eu[:], tile_e[:]))
            nc.vector.tensor_copy(tile_ru[:], tile_r[:]).then_inc(table_ok, 1)
            dve.wait_ge(table_ok, 1)

            def tile_w1(j, i, first):
                e = dve.value_load(tile_eu[0:1, bass.ds(j, 1)], min_val=0, max_val=E - 1)
                if not first:
                    dve.wait_ge(f_h, j - 1)
                nc.vector.tensor_copy(w1t[i], w1_sb[:, bass.ds(e, 1), :, :].rearrange("p e c f -> p (e c) f"))\
                    .then_inc(f_w1, 1)

            def tile_meta(j, i, jj, first):
                dve.wait_ge(f_in[i], 16 * (jj + 1))
                if not first:
                    dve.wait_ge(f_out[i], 16 * jj)
                m, row = ymeta[i], xf[i]
                w_first, w_second, e_first, tok = (row[:, D + k:D + k + 1] for k in range(4))
                nc.vector.tensor_tensor(m[:, 0:1], tile_e[:, bass.ds(j, 1)], e_first, ALU.is_equal)
                nc.vector.tensor_scalar(m[:, 4:5], tok, float(TOK), float(i * P), ALU.is_ge, ALU.mult)
                link(nc.vector.tensor_tensor(m[:, 1:2], w_first, w_second, ALU.subtract))
                nc.vector.tensor_scalar(m[:, 3:4], m[:, 0:1], -float(RESULTS), float(RESULTS), ALU.mult, ALU.add)
                nc.vector.tensor_tensor(m[:, 5:6], m[:, 4:5], tok, ALU.add)
                link(nc.vector.scalar_tensor_tensor(m[:, 2:3], m[:, 1:2], m[:, 0:1], w_second, ALU.mult, ALU.add))
                link(nc.vector.tensor_tensor(ydest[i][:], m[:, 3:4], m[:, 5:6], ALU.add))

            def tiles(jj, base_, first, last):
                chain[:] = [0, base_]
                for i in range(TB):
                    j = TB * jj + i
                    if not last or i < TB - 2:
                        tile_w1(j + 2, i % 2, False)
                    if not last or i < TB - 1:
                        tile_meta(j + 1, (i + 1) % TB, jj + (i + 1) // TB, first and i < TB - 1)
                    dve.wait_ge(f_y, j + 1)
                    nc.vector.tensor_scalar(ys[i], banks[6 + i % 2][:, 0:D], ymeta[i][:, 2:3], None, ALU.mult).then_inc(f_ys, 1)

            dve.wait_ge(w1_in, 16 * E)
            tile_w1(0, 0, True)
            tile_w1(1, 1, True)
            tile_meta(0, 0, 0, True)
            links0 = chain[1] + chain[0] 
            tiles(0, links0, True, False)
            with dve.Fori(1, TILES // TB - 1) as jj:
                tiles(jj, links0 + META_LINKS * TB * jj, False, False)
            tiles(TILES // TB - 1, links0 + META_LINKS * TB * (TILES // TB - 1), False, True)
            links1 = chain[1] + chain[0]

            def result(k, i, kk):
                dve.wait_ge(e_in[i], 32 * (kk + 1))
                y2 = xy[:, bass.ds(2 * k, 2), :].rearrange("p u d -> p (u d)")
                nc.vector.tensor_tensor(y2, y2, fin[i][0], ALU.add).then_inc(dch, 1)
                dve.wait_ge(dch, links1 + k + 1)
                nc.vector.tensor_tensor(y2, y2, fin[i][1], ALU.add).then_inc(e_add, 1)

            with dve.Fori(0, B // 4) as kk:
                result(2 * kk, 0, kk)
                result(2 * kk + 1, 1, kk)

        def rowid():
            return rowf[:, 0:1]

        @block.tensor
        def _(pe):
            def use(g, u):
                if not isinstance(g, int) or A_USES * g + u >= 2:
                    pe.wait_ge(a_free, A_USES * g + u - 1)
                return a_bank[u % 2]

            def stage_k(g):
                pe.wait_ge(ctx_in, 16 * (g + 1))
                for m in range(KC):
                    bank = use(g, m)
                    for c in range(KC):
                        last = nc.tensor.matmul(bank[:], wk_sb[:, c, m * P:(m + 1) * P], ctxg[:, c, :],
                                                start=c == 0, stop=c == KC - 1)
                    last.then_inc(a_done, 1)

            def stage_q(g):
                pe.wait_ge(xn_ok, g + 1)
                for c in range(KC):
                    bank = use(g, 2 + c)
                    for t in range(T):
                        last = nc.tensor.transpose(bank[:, t * P:(t + 1) * P], xn[:, t, c * P:(c + 1) * P], ident[:])
                    last.then_inc(a_done, 1)
                pe.wait_ge(a_free, A_USES * g + 4)
                for m in range(KC):
                    bank = use(g, 4 + m)
                    for c in range(KC):
                        last = nc.tensor.matmul(bank[:], wq_sb[:, c, m * P:(m + 1) * P], xnT[:, c, :],
                                                start=c == 0, stop=c == KC - 1)
                    last.then_inc(a_done, 1)

            def hidden(g, c, u, pairs):
                pe.wait_ge(a_free, A_USES * g + 6)
                for p in pairs:
                    bank = use(g, u + p)
                    nc.tensor.matmul(bank[:], g1_sb[:, p, :], qT[:, c, :], start=True, stop=True).then_inc(a_done, 1)

            def stage_gate(g, c, u, pairs=range(PAIRS)):
                hidden(g, c, u, pairs)
                gate(g, u)

            def gate(g, u):
                bank = use(g, u + PAIRS)
                for p in range(PAIRS):
                    pe.wait_ge(a_free, A_USES * g + u + p + 1)
                    last = nc.tensor.matmul(bank[2 * DH * p:2 * DH * (p + 1), :], g2_sb[:], hid[:, p, :],
                                            start=True, stop=True)
                last.then_inc(a_done, 1)

            def stage_v(g, ts=range(T)):
                for t in ts:
                    bank = use(g, 16 + t)
                    for c in range(KC):
                        last = nc.tensor.matmul(bank[:, 0:D], ctxg[:, c, t * P:(t + 1) * P], wv_sb[:, c, :],
                                                start=c == 0, stop=c == KC - 1)
                    last.then_inc(a_done, 1)

            def bias(bank, side):
                nc.tensor.matmul(bank[:], identb[:], bias_b[:, side, :].unsqueeze(1).to_broadcast([P, QH, P]),
                                 start=True, stop=False)

            def scores(n, g, par, t, c):
                if not isinstance(n, int) or NQ * n + c >= 2:
                    pe.wait_ge(max_done, NQ * n + c - 1)
                if t == 0 and c == 0:
                    pe.wait_ge(k_st, 16 * NT * (g + 1))
                if t == 0 and c % (NQ // KC) == 0:
                    pe.wait_ge(q_st[c // (NQ // KC)], 16 * NT * (g + 1))
                bank = sq_bank[c % 2]
                bias(bank, 0)
                for j in range(QH):
                    h = QH * c + j
                    last = nc.tensor.matmul(bank[:, j * P:(j + 1) * P], head(par, 0, h, t, KR),
                                            head(par, 1, h, t, KR), start=False, stop=j == QH - 1)
                last.then_inc(s_done, 1)

            def shifted(n, par, t, c):
                if not isinstance(n, int) or NQ * n + c >= 2:
                    pe.wait_ge(exp_done, NQ * n + c - 1)
                if c == 0:
                    pe.wait_ge(m_in, 16 * (n + 1))
                bank = sk_bank[c % 2]
                bias(bank, 1)
                for j in range(QH):
                    h = QH * c + j
                    last = nc.tensor.matmul(bank[:, j * P:(j + 1) * P], head(par, 1, h, t, KR + MR),
                                            head(par, 0, h, t, KR + MR), start=False, stop=j == QH - 1)
                last.then_inc(st_done, 1)

            def values(n, t, c, old1):
                pe.wait_ge(exp_done, NQ * n + c + 1)
                if c == 0 and old1:
                    pe.wait_ge(os_ok, n)
                for j in range(QH):
                    last = nc.tensor.matmul(o_bank[VW * j:VW * (j + 1), c * P:(c + 1) * P], v[:, t, QH * c + j, :],
                                            pT[:, c, j * P:(j + 1) * P], start=True, stop=True)
                last.then_inc(pv_done, 1)

            def max_rows(n):
                pe.wait_ge(m3_ok, n + 1)
                pe.sem_inc(pe_passed, 1)
                return nc.tensor.transpose(mT_ps, m3[:].rearrange("p s h -> p (s h)"), identb[:])

            pe.wait_ge(gelu_b, 1)
            for c in range(KC):
                last = nc.tensor.matmul(o_bank[:, c:c + 1], wb2_sb[:, c * P:(c + 1) * P], wb1g[:], start=True, stop=True)
            last.then_inc(base_mm, 1)
            pe.wait_ge(const_pool, CONST_POOL)
            pe.wait_ge(c_wq, 16)
            pe.wait_ge(c_wk, 16)
            stage_k(0)
            stage_q(0)
            stage_gate(0, 0, 6)
            stage_gate(0, 1, 11)
            pe.wait_ge(c_wv, 16)
            stage_v(0)
            pe.wait_ge(const_dve, 3)
            for c in range(NQ):
                scores(0, 0, 0, 0, c)
            max_rows(0).then_inc(m_done, 1)
            scores(1, 0, 0, 1, 0)
            scores(1, 0, 0, 1, 1)
            pe.wait_ge(c_wo, 16)

            def bank_read(n, now):
                if now:
                    pe.wait_ge(mT_sb, n + 1)
                if not isinstance(n, int) or n >= 3:
                    pe.wait_ge(c_read, n - 2)

            def scores_of(g, par, t, ahead, c):
                over = (t + ahead) // T
                scores(T * g + t + ahead, g + over, par ^ over, (t + ahead) % T, c)

            def slot(g, par, t, a, now, nxt, nxt2, old1, old2):
                n = T * g + t
                for c in range(NQ):
                    if nxt and c < NQ - 2:
                        scores_of(g, par, t, 1, c + 2)
                    if now:
                        shifted(n, par, t, c)
                        if c:
                            values(n, t, c - 1, old1)
                    if c == 0 and old1:
                        pe.wait_ge(os_ok, n)
                        bank_read(n, now)
                        for k in range(NQ):
                            last = nc.tensor.transpose(u_bank[:, k * P:(k + 1) * P], oS[:, k, :], ident[:])
                        last.then_inc(nat_done, 1)
                    if c == 1 and (old1 or old2):
                        if old1:
                            pe.wait_ge(o_ok, n)
                        else:
                            bank_read(n, False)
                        if old2:
                            pe.wait_ge(x2_ok, n - 1)
                        for k in range(2 * KC):
                            of = (o, pay[t % 2])[k // KC]
                            if (old1, old2)[k // KC]:
                                last = nc.tensor.transpose(u_bank[:, k * P:(k + 1) * P], of[:, k % KC * P:(k % KC + 1) * P],
                                                           ident[:])
                        last.then_inc(turn_done, 1)
                if old1 or old2:
                    pe.wait_ge(turn_sb, n)
                    for k in range(KC):
                        if old1:
                            last = nc.tensor.matmul(u_bank[:, 0:D], turned[:, k, :], wo_sb[:, k, :],
                                                    start=k == 0, stop=k == KC - 1)
                    for k in range(KC):
                        if old2:
                            last = nc.tensor.matmul(u_bank[:, D:D + E], turned[:, KC + k, :], wr_sb[:, k, :],
                                                    start=k == 0, stop=k == KC - 1)
                    last.then_inc(lo_done, 1)
                if now:
                    values(n, t, NQ - 1, old1)
                if a and t == 0:
                    stage_k(g + 1)
                if a and t == 1:
                    hidden(g + 1, 1, 11, range(PAIRS // 2))
                if a and t == 3:
                    stage_v(g + 1, (2,))
                if nxt2:
                    scores_of(g, par, t, 2, 0)
                if old1 or old2:
                    pe.wait_ge(lo_read, n)
                else:
                    pe.wait_ge(mT_sb, n + 1)
                if nxt:
                    max_rows(n + 1).then_inc(m_done, 1)
                if a and t == 0:
                    stage_q(g + 1)
                if a and t == 1:
                    hidden(g + 1, 1, 11, range(PAIRS // 2, PAIRS))
                if a and t == 2:
                    stage_v(g + 1, (0,))
                if a and t == 3:
                    stage_v(g + 1, (3,))
                if nxt2:
                    scores_of(g, par, t, 2, 1)
                if old2:
                    pe.wait_ge(hot_ok, n - 1)
                    if nxt:
                        pe.wait_ge(mT_sb, n + 2)
                    nc.tensor.matmul(u_bank[:, D:D + E], before[:], hotb[:], start=True, stop=True)
                    nc.tensor.matmul(u_bank[:, D + E:D + 2 * E], ones_b[:], hotb[:], start=True, stop=True)\
                        .then_inc(c_done, 1)
                if a and t == 0:
                    stage_gate(g + 1, 0, 6)
                if a and t == 1:
                    gate(g + 1, 11)
                if a and t == 2:
                    stage_v(g + 1, (1,))

            for t in range(T):
                slot(0, 0, t, True, True, True, True, t >= 1, t >= 2)
            with pe.Fori(0, (G - 2) // 2) as gg:
                for par in (1, 0):
                    for t in range(T):
                        slot(2 * gg + 2 - par, par, t, True, True, True, True, True, True)
            for t in range(T):
                slot(G - 1, 1, t, False, True, t < T - 1, t < T - 2, True, True)
            slot(G, 0, 0, False, False, False, False, True, True)
            slot(G, 0, 1, False, False, False, False, False, True)

            pe.wait_ge(c_read, B)
            pe.wait_ge(w2_in, 16 * E * T)
            pe.wait_ge(table_ok, 1)

            def tile_x(j, i, k, jj):
                pe.wait_ge(f_in[k], 16 * (jj + 1))
                if not isinstance(j, int) or j >= 2:
                    pe.wait_ge(f_xts, j - 1)
                for c in range(KC):
                    last = nc.tensor.transpose(banks[i][:, c * P:(c + 1) * P], xf[k][:, c * P:(c + 1) * P], ident[:])
                last.then_inc(f_xt, 1)

            def tile_h(j, i):
                pe.wait_ge(f_xts, j + 1)
                pe.wait_ge(f_w1, j + 1)
                if not isinstance(j, int) or j >= 2:
                    pe.wait_ge(f_hs, j - 1)
                for f in range(FC):
                    for c in range(KC):
                        last = nc.tensor.matmul(banks[2 + i][:, f * P:(f + 1) * P], w1t[i][:, c, f * P:(f + 1) * P],
                                                xfT[i][:, c, :], start=c == 0, stop=c == KC - 1)
                last.then_inc(f_h, 1)

            def tile_y(j, i):
                e = pe.value_load(tile_eu[0:1, bass.ds(j, 1)], min_val=0, max_val=E - 1)
                pe.wait_ge(f_hs, j + 1)
                if not isinstance(j, int) or j >= 2:
                    pe.wait_ge(f_ys, j - 1)
                for f in range(FC):
                    last = nc.tensor.matmul(banks[6 + i][:, 0:D], hT[i][:, f * P:(f + 1) * P],
                                            w2_sb[:, bass.ds(e, 1), f, :].rearrange("p e f -> p (e f)"),
                                            start=f == 0, stop=f == FC - 1)
                last.then_inc(f_y, 1)

            def tiles(jj, last):
                for i in range(TB):
                    j = TB * jj + i
                    if not last or i < TB - 2:
                        tile_x(j + 2, i % 2, (i + 2) % TB, jj + (i + 2) // TB)
                    if not last or i < TB - 1:
                        tile_h(j + 1, (i + 1) % 2)
                    tile_y(j, i % 2)

            tile_x(0, 0, 0, 0)
            tile_x(1, 1, 1, 0)
            tile_h(0, 0)
            tiles(0, False)
            with pe.Fori(1, TILES // TB - 1) as jj:
                tiles(jj, False)
            tiles(TILES // TB - 1, True)


_INS = ["x", "ctxT", "mask", "maskT", "gx", "gf", "wqT", "wkT", "wvT", "woT", "wb1", "wb2T", "gate1", "gate2",
        "wr", "w1", "w2"]


def kernel(x, ctx_1024, mask_1x1xSxS2_bf1, g_xattn, g_ffn, L0_xattn_wq, L0_xattn_wk, L0_xattn_wv, L0_xattn_wo,
           L0_xattn_wb1, L0_xattn_wb2, L0_xattn_wg1, L0_xattn_wg2, L0_ffn_router_w, L0_ffn_w1, L0_ffn_w2):
    import numpy as np
    import concourse.bacc as bacc
    from concourse.bass_utils import run_bass_kernel_spmd

    mask = np.asarray(mask_1x1xSxS2_bf1)[0, 0].view(np.uint8)
    wg1, wg2 = np.asarray(L0_xattn_wg1), np.asarray(L0_xattn_wg2)
    gate1 = np.zeros((P, PAIRS, P), np.float32)
    gate2 = np.zeros((P, 2 * DH), np.float32)
    for a in range(2):
        for pair in range(PAIRS):
            row = 2 * DH * pair + DH * a
            gate1[row:row + DH, pair, HID * a:HID * (a + 1)] = wg1.T
        gate2[HID * a:HID * (a + 1), DH * a:DH * (a + 1)] = wg2.T
    arrays = {
        "x": np.asarray(x),
        "ctxT": np.asarray(ctx_1024).reshape(TOK, D).T,
        "mask": mask,
        "maskT": mask.T,
        "gx": np.asarray(g_xattn).reshape(1, 1),
        "gf": np.asarray(g_ffn).reshape(1, 1),
        "wqT": np.asarray(L0_xattn_wq).T,
        "wkT": np.asarray(L0_xattn_wk).T,
        "wvT": np.asarray(L0_xattn_wv).T,
        "woT": np.asarray(L0_xattn_wo).T,
        "wb1": np.asarray(L0_xattn_wb1),
        "wb2T": np.asarray(L0_xattn_wb2).T,
        "gate1": gate1,
        "gate2": gate2,
        "wr": np.asarray(L0_ffn_router_w),
        "w1": np.asarray(L0_ffn_w1),
        "w2": np.asarray(L0_ffn_w2),
    }
    nc = bacc.Bacc("TRN2", target_bir_lowering=False, num_devices=1)
    args = []
    for name in _INS:
        arrays[name] = np.ascontiguousarray(arrays[name])
        a = arrays[name]
        args.append(nc.dram_tensor(f"in_{name}", a.shape, mybir.dt.from_np(a.dtype), kind="ExternalInput").ap())
    args.append(nc.dram_tensor("out_0", (B, S, D), F32, kind="ExternalOutput").ap())
    build(nc, *args)
    got = run_bass_kernel_spmd(nc, [{f"in_{n}": arrays[n] for n in _INS}], core_ids=[0])
    return got.results[0]["out_0"]
```

```python
import math

import concourse.bass as bass
from concourse import mybir
from concourse.alu_op_type import AluOpType as ALU

F32 = mybir.dt.float32
BF16 = mybir.dt.bfloat16
U32 = mybir.dt.uint32
U8 = mybir.dt.uint8
ACT = mybir.ActivationFunctionType
AX = mybir.AxisListType

B, S, D = 32, 128, 256
H, DH = 16, 16
P = 128
T = 4
G = B // T
GT = T * S
KC = D // P
HC = H // KC
HID = 64
PAIRS = HC // 2
QH = 4
NQ = H // QH
TERMS_Q = (0, 0, 1, 0, 2, 1)
TERMS_K = (0, 1, 0, 2, 0, 1)
NT = len(TERMS_Q)
KR = NT * DH
MR = 3
VW = 32
TWO_ONES = 1.0 + 0x3f80 * 2.0 ** -23
NEG = -float(2.0 ** 100)
N_CONTEXT = 512
E, F = 8, 512
FC = F // P
TOK = B * S
REGION = TOK + P
TILES = 72
SPARE = TILES - 2 * TOK // P
TB = 4
RB = 8
RESULTS = TOK + TB * P
PW = D + 4
PAD_ROWS = E * REGION
A_USES = 20
EPS = 1e-5
SMALL = 9
CONST_IDENT, CONST_MATRICES, CONST_POOL = 4, 10, 19
META_LINKS = 3
ROUTE = 3
LINKS = 58


def build(nc, x, ctxT, mask, maskT, gx, gf, wqT, wkT, wvT, woT, wb1, wb2T, gate1, gate2, wr, w1, w2, out):
    from contextlib import ExitStack

    x_t = x.rearrange("b s d -> s b d")
    ctx_t = ctxT.rearrange("(c p) t -> p c t", p=P)
    out_t = out.rearrange("b s d -> s b d")

    ctx = ExitStack()
    with ctx:
        def sb(name, shape, dt=F32):
            return ctx.enter_context(nc.sbuf_tensor(name, shape, dt))

        def sem(name):
            return ctx.enter_context(nc.semaphore(name))

        kparts_d = nc.dram_tensor("kparts_d", [D, 3, GT], BF16, kind="Internal").ap()
        qparts_d = nc.dram_tensor("qparts_d", [D, 3, GT], BF16, kind="Internal").ap()
        rows_d = nc.dram_tensor("rows_d", [E * REGION + SPARE * P, PW], F32, kind="Internal").ap()
        ffn_d = nc.dram_tensor("ffn_d", [2 * RESULTS, D], F32, kind="Internal").ap()

        xy = sb("xy", [P, B, D])
        stack = sb("stack", [P, 2, 2, H, GT], BF16)
        w1_sb = stack[:, 0, :, :, :].rearrange("p a h t -> p (a h t)").bitcast(F32)\
            .rearrange("p (e c f) -> p e c f", e=E, c=KC)
        w2_sb = stack[:, 1, :, :, :].rearrange("p a h t -> p (a h t)").bitcast(F32)\
            .rearrange("p (e c f) -> p e c f", e=E, c=FC)
        ident = sb("ident", [P, P])
        identb = sb("identb", [P, P], BF16)
        ones_b = sb("ones_b", [P, P], BF16)
        before = sb("before", [P, P], BF16)
        mask_u = sb("mask_u", [P, 2, P], U8)
        bias_b = sb("bias_b", [P, 2, P], BF16)
        seen = sb("seen", [P, 4])
        gates = sb("gates", [P, 2])
        graw = sb("graw", [P, 2])
        wq_sb, wk_sb, wv_sb, wo_sb = (sb(n, [P, KC, D]) for n in ("wq_sb", "wk_sb", "wv_sb", "wo_sb"))
        g1_sb = sb("g1_sb", [P, PAIRS, P])
        g2_sb = sb("g2_sb", [P, 2 * DH])
        wr_sb = sb("wr_sb", [P, KC, E])
        wb1_sb = sb("wb1_sb", [HID, 1])
        wb1g = sb("wb1g", [HID, 1])
        wb2_sb = sb("wb2_sb", [HID, D])
        base = sb("base", [P, KC])
        ctxg = sb("ctxg", [P, KC, GT])
        xn = sb("xn", [P, T, D])
        xnT = sb("xnT", [P, KC, GT])
        qT = sb("qT", [P, KC, GT])
        kT = sb("kT", [P, KC, GT])
        th = sb("th", [P, KC, GT])
        hid = sb("hid", [P, PAIRS, GT])
        rest = sb("rest", [P, GT])
        krest = sb("krest", [P, GT])
        q3 = sb("q3", [P, KC, 3, GT], BF16)
        k3 = sb("k3", [P, KC, 3, GT], BF16)
        v = sb("v", [P, T, H, VW])
        pT = sb("pT", [P, NQ, QH * P])
        stats = sb("stats", [P, T, 6])
        mv = sb("mv", [P, T, 2])
        rstd = sb("rstd", [P, T])
        half = sb("half", [P, T])
        minus1 = sb("minus1", [P, 1])
        m_neg = sb("m_neg", [P, H])
        m_rest = sb("m_rest", [P, H])
        m3 = sb("m3", [P, MR, H], BF16)
        m3T = sb("m3T", [MR * H, P], BF16)
        oS = sb("oS", [P, NQ, P])
        rden = sb("rden", [P, H])
        o = sb("o", [P, D])
        turned = sb("turned", [P, 2 * KC, P])
        stats2 = sb("stats2", [P, 6])
        mv2 = sb("mv2", [P, 2])
        rstd2 = sb("rstd2", [P, 1])
        pay = [sb(f"pay{i}", [P, PW]) for i in range(2)]
        dest = [sb(f"dest{i}", [P, 2], U32) for i in range(2)]
        logit = sb("logit", [P, E])
        top = sb("top", [P, E])
        topi = sb("topi", [P, E], U32)
        topf = sb("topf", [P, 2])
        r1 = sb("r1", [P, 4])
        hot = sb("hot", [P, 2, E])
        hotb = sb("hotb", [P, E], BF16)
        iota8 = sb("iota8", [P, E])
        count = sb("count", [P, E])
        pos = sb("pos", [P, 3, E])
        destf = sb("destf", [P, 2])
        tokid = sb("tokid", [P, 1])
        nrow = sb("nrow", [P, E, 32])
        thr = sb("thr", [P, E, 32])
        ntile = sb("ntile", [P, E])
        ends = sb("ends", [P, E])
        jump = sb("jump", [P, E])
        iotaj = sb("iotaj", [P, TILES])
        past = sb("past", [P, TILES, E])
        jumps = sb("jumps", [P, TILES, E])
        upto = sb("upto", [P, E, E])
        later = sb("later", [P, E, E])
        tile_e = sb("tile_e", [P, TILES])
        tile_r = sb("tile_r", [P, TILES])
        tile_eu = sb("tile_eu", [P, TILES], U32)
        tile_ru = sb("tile_ru", [P, TILES], U32)
        padi = sb("padi", [P, E], U32)
        zrow = sb("zrow", [P, PW])
        xf = [(q3, k3)[i // 2][:, i % 2, :, :].rearrange("p a t -> p (a t)").bitcast(F32)[:, 0:PW] for i in range(TB)]
        xfT = [xnT[:, i, 0:D].rearrange("p (c t) -> p c t", c=KC) for i in range(2)]
        hT = [qT[:, i, :] for i in range(2)]
        w1t = [hid[:, KC * i:KC * (i + 1), :] for i in range(2)]
        ys = [th[:, i // 2, i % 2 * D:(i % 2 + 1) * D] for i in range(TB)]
        ymeta = [sb(f"ymeta{i}", [P, 6]) for i in range(TB)]
        ydest = [sb(f"ydest{i}", [P, 1], U32) for i in range(TB)]
        fin = [stack[:, 0, i // (RB // 2), :, :].rearrange("p h t -> p (h t)").bitcast(F32)
               .rearrange("p (i s d) -> p i s d", i=RB // 2, s=2)[:, i % (RB // 2), :, 0:2 * D] for i in range(RB)]

        banks = [ctx.enter_context(nc.psum_tensor(f"bank{i}", [P, 512], F32)) for i in range(8)]
        sq_bank, sk_bank, a_bank, o_bank, u_bank = banks[0:2], banks[2:4], banks[4:6], banks[6], banks[7]
        mT_ps = u_bank[0:MR * H, 0:P // 2].bitcast(BF16)

        c_wq, c_wk, c_wv, c_wo = sem("wq_loaded"), sem("wk_loaded"), sem("wv_loaded"), sem("wo_loaded")
        c_small = sem("small_loaded")
        c_x0, c_x1, c_x = sem("x_first_loaded"), sem("x_second_loaded"), sem("x_rest_loaded")
        ctx_in = sem("ctx_loaded")
        w1_in, w2_in = sem("w1_loaded"), sem("w2_loaded")
        const_pool, const_dve = sem("pool_constants"), sem("dve_constants")
        gelu_b, base_mm = sem("wb1_gelu"), sem("base_product")
        gates_ok = sem("gates_ready")
        ln_var, ln_rstd, xn_ok = sem("ln_variance"), sem("ln_rstd"), sem("xn_ready")
        a_done, a_free = sem("projection_done"), sem("projection_read")
        q_high, q_high_st = sem("q_high_part_ready"), sem("q_high_part_stored")
        q3_ok, k3_ok = sem("q_parts_ready"), sem("k_parts_ready")
        qb, kb = sem("q_parts_stored"), sem("k_parts_stored")
        q_st = [sem("q_stack_low_heads"), sem("q_stack_high_heads")]
        k_st, k3_high = sem("k_stack_loaded"), sem("k_high_parts")
        s_done, max_done = sem("scores_done"), sem("max_done")
        m3_ok, mT_sb, m_in = sem("max_parts"), sem("max_copied"), sem("max_rows_loaded")
        st_done, exp_done, pv_done = sem("shifted_scores_done"), sem("exp_done"), sem("pv_done")
        os_ok, nat_done, o_ok = sem("strips_copied"), sem("strips_transposed"), sem("o_ready")
        turn_done, turn_sb = sem("turned_done"), sem("turned_ready")
        lo_done, lo_read = sem("output_and_logits_done"), sem("output_and_logits_read")
        m_done = sem("max_turned")
        c_done, c_read = sem("counts_done"), sem("counts_read")
        l2_var, l2_rstd, x2_ok = sem("ln2_variance"), sem("ln2_rstd"), sem("x2_ready")
        gap_ok, gap_exp = sem("gap_ready"), sem("gap_exp")
        hot_ok = sem("hot_ready")
        dest_ok, rows_ok = sem("weights_ready"), sem("row_numbers_ready")
        sc = [sem("rows_sent_even"), sem("rows_sent_odd")]
        pad_ok, pad_in, spare_in = sem("padding_index"), sem("padding_sent"), sem("spare_tiles_sent")
        table_ok = sem("tile_table")
        sp_passed, pool_passed, dve_passed, pe_passed = (sem(n) for n in ("sp_passed", "pool_passed", "dve_passed", "pe_passed"))
        dch, pch, rch = sem("dve_chain"), sem("k_split_chain"), sem("routing_chain")
        f_in = [sem(f"tile_loaded_{i}") for i in range(TB)]
        f_xt, f_xts = sem("tile_transposed"), sem("tile_xT_ready")
        f_h, f_hs = sem("hidden_done"), sem("hidden_silu")
        f_w1 = sem("w1_of_tile")
        f_y, f_ys = sem("tile_product"), sem("tile_scaled")
        f_out = [sem(f"tile_sent_{i}") for i in range(TB)]
        e_in = [sem(f"result_parts_{i}") for i in range(RB)]
        e_add = sem("result_added")
        e_out = sem("result_stored")

        block = ctx.enter_context(nc.Block())

        def head(par, side, h, t, rows):
            return stack[0:rows, par, side, h, t * P:(t + 1) * P]

        def pad_regions(eng, experts):
            eng.wait_ge(pad_ok, 1)
            for e in experts:
                row = eng.value_load(padi[0:1, e:e + 1], min_val=0, max_val=E * REGION - P)
                eng.dma_start(rows_d[bass.ds(row, P), :], zrow[:]).then_inc(pad_in, 16)

        @block.sync
        def _(sp):
            sp.dma_start(ctxg[:], ctx_t[:, :, 0:GT]).then_inc(ctx_in, 16)
            for w_sb, w, c in ((wk_sb, wkT, c_wk), (wq_sb, wqT, c_wq)):
                sp.dma_start(w_sb[:], w.rearrange("(c p) n -> p c n", p=P)).then_inc(c, 16)
            small = (
                (wb1_sb[:], wb1), (wb2_sb[:], wb2T), (g1_sb[:], gate1), (g2_sb[:], gate2),
                (mask_u[:, 0, :], mask), (mask_u[:, 1, :], maskT),
                (graw[:, 0:1], gx.broadcast_to([P, 1])), (graw[:, 1:2], gf.broadcast_to([P, 1])),
                (wr_sb[:], wr.rearrange("(c p) e -> p c e", p=P)),
            )
            assert len(small) == SMALL
            for to, of in small:
                sp.dma_start(to, of).then_inc(c_small, 16)
            for w_sb, w, c in ((wv_sb, wvT, c_wv), (wo_sb, woT, c_wo)):
                sp.dma_start(w_sb[:], w.rearrange("(c p) n -> p c n", p=P)).then_inc(c, 16)
            sp.dma_start(xy[:, T:2 * T, :], x_t[:, T:2 * T, :]).then_inc(c_x1, 16)
            sp.dma_start(xy[:, 2 * T:B, :], x_t[:, 2 * T:B, :]).then_inc(c_x, 16)

            def store_k(g, first):
                sp.wait_ge(k3_ok, g + 1)
                sp.sem_inc(sp_passed, 1)
                if not first:
                    sp.wait_ge(k_st, 16 * NT * g)
                sp.dma_start(kparts_d.rearrange("(c p) s t -> p c s t", p=P), k3[:]).then_inc(kb, 16)

            def load_k(g, par):
                sp.wait_ge(kb, 16 * (g + 1))
                for j, part in enumerate(TERMS_K):
                    sp.dma_start(stack[DH * j:DH * (j + 1), par, 1, :, :],
                                 kparts_d[:, part, :].rearrange("(h d) t -> d h t", d=DH)).then_inc(k_st, 16)

            def store_q(g, c, first):
                sp.wait_ge(q_high, KC * g + c + 1)
                sp.sem_inc(sp_passed, 1)
                if not first:
                    sp.wait_ge(q_st[c], 16 * NT * g)
                sp.dma_start(qparts_d[c * P:(c + 1) * P, 0, :], q3[:, c, 0, :]).then_inc(q_high_st, 16)
                sp.wait_ge(q3_ok, KC * g + c + 1)
                sp.dma_start(qparts_d[c * P:(c + 1) * P, 1:3, :], q3[:, c, 1:3, :]).then_inc(qb, 16)

            def load_q(g, c, par):
                def term(j):
                    sp.dma_start(stack[DH * j:DH * (j + 1), par, 0, HC * c:HC * (c + 1), :],
                                 qparts_d[c * P:(c + 1) * P, TERMS_Q[j], :].rearrange("(h d) t -> d h t", d=DH))\
                        .then_inc(q_st[c], 16)

                sp.wait_ge(q_high_st, 16 * (KC * g + c + 1))
                for j in range(NT):
                    if TERMS_Q[j] == 0:
                        term(j)
                sp.wait_ge(qb, 16 * (KC * g + c + 1))
                for j in range(NT):
                    if TERMS_Q[j] > 0:
                        term(j)

            def load_max(n, par, t):
                sp.wait_ge(mT_sb, n + 1)
                sp.dma_start(stack[KR:KR + MR, par, 0, :, t * P:(t + 1) * P],
                             m3T[:, :]).then_inc(m_in, 16)

            store_k(0, True)
            store_q(0, 0, True)
            load_k(0, 0)
            load_q(0, 0, 0)
            store_q(0, 1, True)
            load_q(0, 1, 0)
            load_max(0, 0, 0)

            def group(g, par, last):
                n = T * g
                if not last:
                    sp.wait_ge(a_done, A_USES * (g + 1))
                    sp.dma_start(ctxg[:], ctx_t[:, :, bass.ds((g + 1) * GT, GT)]).then_inc(ctx_in, 16)
                load_max(n + 1, par, 1)
                if not last:
                    store_k(g + 1, False)
                    load_k(g + 1, 1 - par)
                load_max(n + 2, par, 2)
                if not last:
                    store_q(g + 1, 0, False)
                    load_q(g + 1, 0, 1 - par)
                    store_q(g + 1, 1, False)
                    load_q(g + 1, 1, 1 - par)
                if last:
                    load_w2(0)
                load_max(n + 3, par, 3)
                if last:
                    load_w2(1)
                else:
                    load_max(n + 4, 1 - par, 0)

            def load_w2(t):
                sp.wait_ge(st_done, NQ * (T * (G - 1) + t + 1))
                cols = slice(D // T * t, D // T * (t + 1))
                for e in range(E):
                    sp.dma_start(w2_sb[:, e, :, cols], w2[e, :, cols].rearrange("(c p) f -> p c f", p=P)).then_inc(w2_in, 16)

            group(0, 0, False)
            with sp.Fori(0, (G - 2) // 2) as gg:
                group(2 * gg + 1, 1, False)
                group(2 * gg + 2, 0, False)
            sp.wait_ge(const_pool, CONST_POOL)
            for i in range(SPARE):
                sp.dma_start(rows_d[PAD_ROWS + i * P:PAD_ROWS + (i + 1) * P, :], zrow[:]).then_inc(spare_in, 16)

            group(G - 1, 1, True)
            load_w2(2)
            load_w2(3)

            pad_regions(sp, range(0, E // 2))

            sp.wait_ge(table_ok, 1)
            sp.wait_ge(sc[0], 32 * B // 2)
            sp.wait_ge(sc[1], 32 * B // 2)
            sp.wait_ge(pad_in, 16 * E)
            sp.wait_ge(spare_in, 16 * SPARE)

            def load_tile(j, i, first):
                row = sp.value_load(tile_ru[0:1, bass.ds(j, 1)], min_val=0, max_val=E * REGION + (SPARE - 1) * P)
                if not first:
                    sp.wait_ge(f_ys, j - TB + 1)
                sp.dma_start(xf[i], rows_d[bass.ds(row, P), :]).then_inc(f_in[i], 16)

            for i in range(TB):
                load_tile(i, i, True)
            sp.wait_ge(table_ok, 2)
            with sp.Fori(1, TILES // TB) as jj:
                for i in range(TB):
                    load_tile(TB * jj + i, i, False)

            for sent in f_out:
                sp.wait_ge(sent, 16 * TILES // TB)

            def load_result(k, i, first):
                if not first:
                    sp.wait_ge(e_add, k - RB + 1)
                    sp.sem_inc(sp_passed, 1)
                for s in range(2):
                    sp.dma_start(fin[i][:, s, :].rearrange("p (u d) -> p u d", d=D),
                                 ffn_d[bass.ds(s * RESULTS + k * 2 * P, 2 * P), :].rearrange("(u p) d -> p u d", p=P))\
                        .then_inc(e_in[i], 16)

            def store_result(k):
                sp.wait_ge(e_add, k + 1)
                sp.sem_inc(sp_passed, 1)
                sp.dma_start(out_t[:, bass.ds(2 * k, 2), :], xy[:, bass.ds(2 * k, 2), :]).then_inc(e_out, 16)

            for i in range(RB):
                load_result(i, i, True)
            with sp.Fori(1, B // 2 // RB) as kk:
                for i in range(RB):
                    store_result(RB * kk - RB + i)
                    load_result(RB * kk + i, i, False)
            for i in range(RB):
                store_result(B // 2 - RB + i)
            sp.wait_ge(e_out, 16 * (B // 2))

        @block.gpsimd
        def _(pool):
            nc.gpsimd.memset(ident[:], 0.0).then_inc(const_pool, 1)
            nc.gpsimd.memset(half[:], -0.5).then_inc(const_pool, 1)
            nc.gpsimd.memset(minus1[:], -1.0).then_inc(const_pool, 1)
            pool.wait_ge(const_pool, 3)
            nc.gpsimd.affine_select(out=ident[:], in_=ident[:], compare_op=ALU.not_equal, fill=1.0, base=0,
                                    pattern=[[-1, P]], channel_multiplier=1).then_inc(const_pool, 1)

            def matrices():
                nc.gpsimd.memset(identb[:], 0.0).then_inc(const_pool, 1)
                nc.gpsimd.memset(before[:], 1.0).then_inc(const_pool, 1)
                nc.gpsimd.memset(v[:], 0.0).then_inc(const_pool, 1)
                pool.wait_ge(const_pool, 7)
                nc.gpsimd.affine_select(out=identb[:], in_=identb[:], compare_op=ALU.not_equal, fill=1.0, base=0,
                                        pattern=[[-1, P]], channel_multiplier=1).then_inc(const_pool, 1)
                nc.gpsimd.affine_select(out=before[:], in_=before[:], compare_op=ALU.is_gt, fill=0.0, base=0,
                                        pattern=[[1, P]], channel_multiplier=-1).then_inc(const_pool, 1)
                nc.gpsimd.memset(v[:, :, :, DH:DH + 1], 1.0).then_inc(const_pool, 1)

            def routing_tables():
                def iota(to, pattern, base, by_row):
                    return nc.gpsimd.iota(to, pattern=pattern, base=base, channel_multiplier=by_row,
                                          allow_small_or_imprecise_dtypes=True)

                iota(iota8[:], [[1, E]], 0, 0).then_inc(const_pool, 1)
                iota(tokid[:], [[0, 1]], 0, 1).then_inc(const_pool, 1)
                iota(count[:], [[REGION, E]], 0, 0).then_inc(const_pool, 1)
                iota(thr[:], [[REGION, E], [P, 32]], 0, 0).then_inc(const_pool, 1)
                iota(iotaj[:], [[1, TILES]], 0, 0).then_inc(const_pool, 1)
                nc.gpsimd.memset(zrow[:], 0.0).then_inc(const_pool, 1)
                nc.gpsimd.memset(later[:], 1.0).then_inc(const_pool, 1)
                pool.wait_ge(const_pool, CONST_POOL - 2)
                nc.gpsimd.affine_select(out=later[:], in_=later[:], compare_op=ALU.is_ge, fill=0.0, base=0,
                                        pattern=[[1, E], [-1, E]], channel_multiplier=0).then_inc(const_pool, 1)
                iota(zrow[:, PW - 1:PW], [[0, 1]], TOK, 1).then_inc(const_pool, 1)

            def rstd_of(g):
                pool.wait_ge(ln_var, g + 1)
                nc.gpsimd.tensor_tensor(rstd[:], mv[:, :, 1], half[:], ALU.pow).then_inc(ln_rstd, 1)

            def split_k(g, first):
                pool.wait_ge(k3_high, g + 1)
                pool.sem_inc(pool_passed, 1)
                pool.wait_ge(a_free, A_USES * g + KC)
                for c in range(KC):
                    w = (3 * KC - 1) * g + 3 * c
                    nc.gpsimd.tensor_tensor(krest[:], kT[:, c, :], k3[:, c, 0, :], ALU.subtract).then_inc(pch, 1)
                    pool.wait_ge(pch, w + 1)
                    pool.sem_inc(pool_passed, 1)
                    nc.gpsimd.tensor_copy(k3[:, c, 1, :], krest[:]).then_inc(pch, 1)
                    pool.wait_ge(pch, w + 2)
                    last = nc.gpsimd.tensor_tensor(k3[:, c, 2, :], krest[:], k3[:, c, 1, :], ALU.subtract)
                    if c < KC - 1:
                        last.then_inc(pch, 1)
                        pool.wait_ge(pch, w + 3)
                last.then_inc(k3_ok, 1)

            def rstd2_of(r):
                pool.wait_ge(l2_var, r + 1)
                nc.gpsimd.tensor_tensor(rstd2[:], mv2[:, 1:2], half[:, 0:1], ALU.pow).then_inc(l2_rstd, 1)

            def weights(r, i):
                pool.wait_ge(gap_exp, r + 1)
                pool.sem_inc(pool_passed, 1)
                nc.gpsimd.tensor_scalar(r1[:, 2:3], r1[:, 1:2], 1.0, None, ALU.add).then_inc(rch, 1)
                pool.wait_ge(rch, ROUTE * r + 1)
                nc.gpsimd.tensor_tensor(r1[:, 3:4], r1[:, 2:3], minus1[:], ALU.pow).then_inc(rch, 1)
                pool.wait_ge(rch, ROUTE * r + 2)
                nc.gpsimd.tensor_tensor(pay[i][:, D:D + 1], r1[:, 3:4], gates[:, 1:2], ALU.mult).then_inc(rch, 1)
                pool.wait_ge(rch, ROUTE * r + 3)
                nc.gpsimd.tensor_tensor(pay[i][:, D + 1:D + 2], pay[i][:, D:D + 1], r1[:, 1:2], ALU.mult)
                nc.gpsimd.tensor_copy(pay[i][:, D + 3:D + 4], tokid[:])
                nc.gpsimd.tensor_scalar(tokid[:], tokid[:], float(S), None, ALU.add)
                pool.wait_ge(rows_ok, r + 1)
                pool.sem_inc(pool_passed, 1)
                nc.gpsimd.tensor_copy(pay[i][:, D + 2:D + 3], topf[:, 0:1])
                nc.gpsimd.tensor_copy(dest[i][:], destf[:]).then_inc(dest_ok, 1)

            def send(r, i):
                pool.wait_ge(dest_ok, r + 1)
                pool.sem_inc(pool_passed, 1)
                for s in range(2):
                    pool.indirect_dma_start(rows_d, bass.IndirectOffsetOnAxis(ap=dest[i][:, s:s + 1], axis=0),
                                            pay[i][:], None).then_inc(sc[i], 16)

            rstd_of(0)
            split_k(0, True)
            matrices()
            routing_tables()

            def slot(g, t, a, old1, old2):
                n = T * g + t
                if a and t == 0:
                    rstd_of(g + 1)
                    split_k(g + 1, False)
                if old1:
                    rstd2_of(n - 1)
                if old2:
                    weights(n - 2, t % 2)
                    send(n - 2, t % 2)

            for t in range(T):
                slot(0, t, True, t >= 1, t >= 2)
            with pool.Fori(1, G - 1) as g:
                for t in range(T):
                    slot(g, t, True, True, True)
            for t in range(T):
                slot(G - 1, t, False, True, True)
            slot(G, 0, False, True, True)
            slot(G, 1, False, False, True)

            def send_tile(j, i):
                pool.wait_ge(f_ys, j + 1)
                pool.sem_inc(pool_passed, 1)
                pool.indirect_dma_start(ffn_d, bass.IndirectOffsetOnAxis(ap=ydest[i][:, 0:1], axis=0),
                                        ys[i], None).then_inc(f_out[i], 16)

            with pool.Fori(0, TILES // TB) as jj:
                for i in range(TB):
                    send_tile(TB * jj + i, i)

        @block.scalar
        def _(act):
            act.dma_start(xy[:, 0:T, :], x_t[:, 0:T, :]).then_inc(c_x0, 16)
            act.wait_ge(c_small, 16 * SMALL)
            nc.scalar.activation(wb1g[:], wb1_sb[:], ACT.Gelu, scale=math.log(N_CONTEXT)).then_inc(gelu_b, 1)
            nc.scalar.activation(gates[:], graw[:], ACT.Tanh).then_inc(gates_ok, 1)

            def evac(g, u, to, func=None):
                act.wait_ge(a_done, A_USES * g + u + 1)
                nc.scalar.activation(to, a_bank[u % 2][:, 0:to_width(to)], func or ACT.Copy).then_inc(a_free, 1)

            def to_width(to):
                return math.prod(to.shape[1:])

            def stage_k(g, first):
                if not first:
                    act.wait_ge(k3_ok, g)
                    act.wait_ge(kb, 16 * g)
                for c in range(KC):
                    act.wait_ge(a_done, A_USES * g + c + 1)
                    last = nc.scalar.activation(k3[:, c, 0, :], a_bank[c][:], ACT.Copy)
                    if c == KC - 1:
                        last.then_inc(k3_high, 1)
                    evac(g, c, kT[:, c, :])

            def stage_q(g, first):
                for c in range(KC):
                    evac(g, 2 + c, xnT[:, c, :])
                if not first:
                    act.wait_ge(q3_ok, KC * g)
                for c in range(KC):
                    evac(g, 4 + c, qT[:, c, :])

            def hidden(g, u):
                for p in range(PAIRS):
                    evac(g, u + p, hid[:, p, :], ACT.Gelu)

            def gate(g, c, u):
                evac(g, u + PAIRS, th[:, c, :], ACT.Tanh)

            def stage_v(g, ts=range(T)):
                for t in ts:
                    act.wait_ge(a_done, A_USES * g + 16 + t + 1)
                    nc.scalar.activation(v[:, t, :, 0:DH],
                                         a_bank[t % 2][:, 0:D].rearrange("p (h d) -> p h d", d=DH),
                                         ACT.Copy).then_inc(a_free, 1)

            stage_k(0, True)
            stage_q(0, True)
            for c, u in ((0, 6), (1, 11)):
                hidden(0, u)
                gate(0, c, u)
            act.wait_ge(const_pool, CONST_MATRICES)
            stage_v(0)

            def slot(g, t, a, now, old1, old2):
                n = T * g + t
                for c in range(NQ):
                    if now:
                        act.wait_ge(st_done, NQ * n + c + 1)
                        if old1:
                            act.wait_ge(pv_done, NQ * (n - 1) + c + 1)
                        nc.scalar.activation(pT[:, c, :], sk_bank[c % 2][:], ACT.Exp).then_inc(exp_done, 1)
                    if c == 1 and (old1 or old2):
                        a0, a1 = 0 if old1 else KC, 2 * KC if old2 else KC
                        act.wait_ge(turn_done, n)
                        nc.scalar.activation(turned[:, a0:a1, :].rearrange("p c t -> p (c t)"),
                                             u_bank[:, a0 * P:a1 * P], ACT.Copy).then_inc(turn_sb, 1)
                if now:
                    act.wait_ge(pv_done, NQ * (n + 1))
                    if old1:
                        act.wait_ge(nat_done, n)
                    nc.scalar.activation(oS[:].rearrange("p c q -> p (c q)"), o_bank[:], ACT.Copy).then_inc(os_ok, 1)
                if a and t == 0:
                    stage_k(g + 1, False)
                    stage_q(g + 1, False)
                    hidden(g + 1, 6)
                if a and t == 1:
                    hidden(g + 1, 11)
                if a and t == 2:
                    stage_v(g + 1, (0,))
                if a and t == 3:
                    stage_v(g + 1, (2,))
                if old2:
                    act.wait_ge(gap_ok, n - 1)
                    nc.scalar.activation(r1[:, 1:2], r1[:, 0:1], ACT.Exp).then_inc(gap_exp, 1)
                if a and t == 0:
                    gate(g + 1, 0, 6)
                if a and t == 1:
                    gate(g + 1, 1, 11)
                if a and t == 2:
                    stage_v(g + 1, (1,))
                if a and t == 3:
                    stage_v(g + 1, (3,))

            for t in range(T):
                slot(0, t, True, True, t >= 1, t >= 2)
            with act.Fori(1, G - 1) as g:
                for t in range(T):
                    slot(g, t, True, True, True, True)
            act.wait_ge(st_done, NQ * T * (G - 1))
            for e in range(E):
                act.dma_start(w1_sb[:, e, :, :], w1[e, :, :].rearrange("(c p) f -> p c f", p=P)).then_inc(w1_in, 16)
            for t in range(T):
                slot(G - 1, t, False, True, True, True)
            slot(G, 0, False, False, True, True)
            slot(G, 1, False, False, False, True)

            def tile_x(j, i):
                act.wait_ge(f_xt, j + 1)
                nc.scalar.activation(xfT[i].rearrange("p c t -> p (c t)"), banks[i][:, 0:D], ACT.Copy).then_inc(f_xts, 1)

            def tile_h(j, i):
                act.wait_ge(f_h, j + 1)
                nc.scalar.activation(hT[i], banks[2 + i][:], ACT.Silu).then_inc(f_hs, 1)

            def tiles(jj, last):
                for i in range(TB):
                    j = TB * jj + i
                    if not last or i < TB - 2:
                        tile_x(j + 2, i % 2)
                    if not last or i < TB - 1:
                        tile_h(j + 1, (i + 1) % 2)

            pad_regions(act, range(E // 2, E))
            tile_x(0, 0)
            tile_x(1, 1)
            tile_h(0, 0)
            with act.Fori(0, TILES // TB - 1) as jj:
                tiles(jj, False)
            tiles(TILES // TB - 1, True)

        @block.vector
        def _(dve):
            chain = [0, 0]

            def link(ins):
                chain[0] += 1
                ins.then_inc(dch, 1)
                dve.wait_ge(dch, chain[1] + chain[0])

            def layer_norm_stats(g):
                for t in range(T):
                    link(nc.vector.bn_stats(stats[:, t, :], xy[:, T * g + t, :]))
                for t in range(T):
                    dve.sem_inc(dve_passed, 1)
                    link(nc.vector.bn_aggr(mv[:, t, :], stats[:, t, :]))
                nc.vector.tensor_scalar(mv[:, :, 1], mv[:, :, 1], EPS, None, ALU.add).then_inc(ln_var, 1)

            def layer_norm(g, first):
                dve.wait_ge(ln_rstd, g + 1)
                if not first:
                    dve.wait_ge(a_done, A_USES * (g - 1) + 4)
                for t in range(T):
                    ins = nc.vector.tensor_scalar(xn[:, t, :], xy[:, T * g + t, :], mv[:, t, 0:1], rstd[:, t:t + 1],
                                                  ALU.subtract, ALU.mult)
                ins.then_inc(xn_ok, 1)

            def q_parts(g, c, first):
                dve.wait_ge(a_free, A_USES * g + (11 if c == 0 else 16))
                if not first:
                    dve.wait_ge(q_high_st, 16 * (KC * g - (KC - 1 - c)))
                    dve.wait_ge(qb, 16 * (KC * g - (KC - 1 - c)))
                link(nc.vector.scalar_tensor_tensor(qT[:, c, :], th[:, c, :], 1.0, qT[:, c, :], ALU.add, ALU.mult))
                nc.vector.tensor_scalar(q3[:, c, 0, :], qT[:, c, :], base[:, c:c + 1], None, ALU.mult).then_inc(q_high, 1)
                dve.wait_ge(q_high, KC * g + c + 1)
                link(nc.vector.scalar_tensor_tensor(rest[:], qT[:, c, :], base[:, c:c + 1], q3[:, c, 0, :],
                                                    ALU.mult, ALU.subtract))
                link(nc.vector.tensor_copy(q3[:, c, 1, :], rest[:]))
                ins = nc.vector.tensor_tensor(q3[:, c, 2, :], rest[:], q3[:, c, 1, :], ALU.subtract)
                ins.then_inc(q3_ok, 1)
                if c == 0:
                    dve.wait_ge(q3_ok, KC * g + 1)

            def row_max(n, c):
                dve.wait_ge(s_done, NQ * n + c + 1)
                nc.vector.tensor_reduce(m_neg[:, QH * c:QH * (c + 1)],
                                        sq_bank[c % 2][:].rearrange("p (h k) -> p h k", h=QH),
                                        axis=AX.X, op=ALU.max, negate=True).then_inc(max_done, 1)

            def max_parts(n, first):
                dve.wait_ge(max_done, NQ * (n + 1))
                if not first:
                    dve.wait_ge(m_done, n)
                link(nc.vector.tensor_copy(m3[:, 0, :], m_neg[:]))
                link(nc.vector.tensor_tensor(m_rest[:], m_neg[:], m3[:, 0, :], ALU.subtract))
                link(nc.vector.tensor_copy(m3[:, 1, :], m_rest[:]))
                nc.vector.tensor_tensor(m3[:, 2, :], m_rest[:], m3[:, 1, :], ALU.subtract).then_inc(m3_ok, 1)

            def copy_max(n, first):
                dve.wait_ge(m_done, n + 1)
                if not first:
                    dve.wait_ge(m_in, 16 * n)
                nc.vector.tensor_copy(m3T[:], mT_ps).then_inc(mT_sb, 1)

            nc.vector.memset(stack[KR:KR + MR, 0, 1, :, :].bitcast(F32), TWO_ONES).then_inc(const_dve, 1)
            dve.wait_ge(c_x0, 16)
            layer_norm_stats(0)
            layer_norm(0, True)
            nc.vector.memset(ones_b[:], 1.0).then_inc(const_dve, 1)
            nc.vector.memset(stack[KR:KR + MR, 1, 1, :, :].bitcast(F32), TWO_ONES).then_inc(const_dve, 1)
            dve.wait_ge(c_small, 16 * SMALL)
            link(nc.vector.tensor_scalar(bias_b[:], mask_u[:], -NEG, NEG, ALU.mult, ALU.add))
            link(nc.vector.tensor_reduce(seen[:, 0:1], mask_u[:, 0, :], axis=AX.X, op=ALU.max))
            link(nc.vector.reciprocal(seen[:, 1:2], seen[:, 0:1]))
            link(nc.vector.tensor_tensor(seen[:, 2:3], seen[:, 0:1], seen[:, 1:2], ALU.mult))
            dve.wait_ge(gates_ok, 1)
            nc.vector.tensor_tensor(seen[:, 3:4], seen[:, 2:3], gates[:, 0:1], ALU.mult).then_inc(const_dve, 1)
            dve.wait_ge(base_mm, 1)
            link(nc.vector.tensor_scalar(base[:], o_bank[:, 0:KC], DH ** -0.5, None, ALU.mult))
            q_parts(0, 0, True)
            q_parts(0, 1, True)
            for c in range(NQ):
                row_max(0, c)
            max_parts(0, True)
            copy_max(0, True)
            row_max(1, 0)
            dve.wait_ge(mT_sb, 1)

            dve.wait_ge(const_pool, CONST_POOL)
            dve.wait_ge(const_dve, 4)
            dve.wait_ge(c_x1, 16)

            def statistics2(r):
                link(nc.vector.bn_stats(stats2[:], xy[:, r, :]))
                dve.sem_inc(dve_passed, 1)
                link(nc.vector.bn_aggr(mv2[:], stats2[:]))
                nc.vector.tensor_scalar(mv2[:, 1:2], mv2[:, 1:2], EPS, None, ALU.add).then_inc(l2_var, 1)

            def slot(g, t, a, nxt, nxt2, old1, old2):
                n = T * g + t
                for c in range(NQ):
                    if nxt and c < NQ - 1:
                        row_max(n + 1, c + 1)
                    if c == 0 and old2:
                        normalise2(n - 2, t % 2, 2 * g + t // 2 - 1, not isinstance(n, int) or n >= 4)
                    if c == 0 and old1:
                        dve.wait_ge(nat_done, n)
                        if old2:
                            dve.wait_ge(turn_done, n - 1)
                        strips = u_bank[:].rearrange("p (h w) -> p h w", w=VW)
                        link(nc.vector.reciprocal(rden[:], strips[:, :, DH]))
                        nc.vector.tensor_tensor(o[:].rearrange("p (h d) -> p h d", d=DH), strips[:, :, 0:DH],
                                                rden[:].unsqueeze(2).to_broadcast([P, H, DH]), ALU.mult).then_inc(o_ok, 1)
                    if c == 0 and a and t == 0:
                        layer_norm_stats(g + 1)
                    if c == 1 and a and t == 0:
                        layer_norm(g + 1, False)
                    if c == 1 and a and t == 1:
                        q_parts(g + 1, 0, False)
                    if c == 0 and a and t == 2:
                        q_parts(g + 1, 1, False)
                if nxt:
                    max_parts(n + 1, False)
                if old1 or old2:
                    dve.wait_ge(lo_done, n)
                    if old1:
                        last = nc.vector.scalar_tensor_tensor(xy[:, n - 1, :], u_bank[:, 0:D], seen[:, 3:4],
                                                              xy[:, n - 1, :], ALU.mult, ALU.add)
                    if old2:
                        last = nc.vector.tensor_copy(logit[:], u_bank[:, D:D + E])
                    last.then_inc(lo_read, 1)
                    dve.wait_ge(lo_read, n)
                if nxt:
                    copy_max(n + 1, False)
                if old1 and not nxt:
                    statistics2(n - 1)
                if old2:
                    if not isinstance(n, int) or n >= 3:
                        dve.wait_ge(dest_ok, n - 2)
                    experts_of(n - 2)
                if nxt2:
                    row_max(n + 2, 0)
                if old2:
                    dve.wait_ge(c_done, n - 1)
                    nc.vector.tensor_tensor(pos[:, 0, :], u_bank[:, D:D + E], count[:], ALU.add)
                    nc.vector.tensor_tensor(count[:], u_bank[:, D + E:D + 2 * E], count[:], ALU.add).then_inc(c_read, 1)
                    dve.wait_ge(c_read, n - 1)
                    link(nc.vector.tensor_tensor(pos[:, 1:3, :], pos[:, 0:1, :].to_broadcast([P, 2, E]), hot[:, 0:2, :],
                                                 ALU.mult))
                    nc.vector.tensor_reduce(destf[:], pos[:, 1:3, :], axis=AX.X, op=ALU.add).then_inc(rows_ok, 1)
                if old1 and nxt:
                    statistics2(n - 1)

            def normalise2(r, i, kth, reused):
                dve.wait_ge(l2_rstd, r + 1)
                if reused:
                    dve.wait_ge(sc[i], 32 * kth)
                nc.vector.tensor_scalar(pay[i][:, 0:D], xy[:, r, :], mv2[:, 0:1], rstd2[:, 0:1],
                                        ALU.subtract, ALU.mult).then_inc(x2_ok, 1)

            def experts_of(r):
                dve.sem_inc(dve_passed, 1)
                link(nc.vector.max(top[:], logit[:]))
                nc.vector.tensor_tensor(r1[:, 0:1], top[:, 1:2], top[:, 0:1], ALU.subtract).then_inc(gap_ok, 1)
                link(nc.vector.max_index(topi[:], top[:], logit[:]))
                link(nc.vector.tensor_copy(topf[:], topi[:, 0:2]))
                for s in range(2):
                    ins = nc.vector.tensor_scalar(hot[:, s, :], iota8[:], topf[:, s:s + 1], None, ALU.is_equal)
                link(ins)
                nc.vector.tensor_tensor(hotb[:], hot[:, 0, :], hot[:, 1, :], ALU.add).then_inc(hot_ok, 1)

            for t in range(T):
                slot(0, t, True, True, True, t >= 1, t >= 2)
            first_links = chain[0]
            dve.wait_ge(c_x, 16)
            with dve.Fori(1, G - 1) as g:
                chain[:] = [0, first_links + (g - 1) * LINKS]
                for t in range(T):
                    slot(g, t, True, True, True, True, True)
                assert chain[0] == LINKS, chain[0]
            chain[:] = [0, first_links + (G - 2) * LINKS]
            for t in range(T):
                slot(G - 1, t, False, t < T - 1, t < T - 2, True, True)
            slot(G, 0, False, False, False, True, True)
            slot(G, 1, False, False, False, False, True)

            nc.vector.tensor_copy(padi[:], count[:]).then_inc(pad_ok, 1)
            link(nc.vector.tensor_tensor(nrow[:], count[:].unsqueeze(2).to_broadcast([P, E, 32]), thr[:], ALU.is_gt))
            link(nc.vector.tensor_reduce(ntile[:], nrow[:], axis=AX.X, op=ALU.add))
            link(nc.vector.tensor_tensor(upto[:], ntile[:].unsqueeze(1).to_broadcast([P, E, E]), later[:], ALU.mult))
            nc.vector.tensor_scalar(jump[:], ntile[:], -float(P), float(REGION), ALU.mult, ALU.add)
            link(nc.vector.tensor_reduce(ends[:], upto[:], axis=AX.X, op=ALU.add))
            for js in (slice(0, 2 * TB), slice(2 * TB, TILES)):
                width = js.stop - js.start
                link(nc.vector.tensor_tensor(past[:, js, :], iotaj[:, js].unsqueeze(2).to_broadcast([P, width, E]),
                                             ends[:].unsqueeze(1).to_broadcast([P, width, E]), ALU.is_ge))
                nc.vector.tensor_reduce(tile_e[:, js], past[:, js, :], axis=AX.X, op=ALU.add)
                link(nc.vector.tensor_tensor(jumps[:, js, :], past[:, js, :],
                                             jump[:].unsqueeze(1).to_broadcast([P, width, E]), ALU.mult))
                nc.vector.tensor_scalar(tile_e[:, js], tile_e[:, js], float(E - 1), None, ALU.min)
                link(nc.vector.tensor_reduce(tile_r[:, js], jumps[:, js, :], axis=AX.X, op=ALU.add))
                link(nc.vector.scalar_tensor_tensor(tile_r[:, js], iotaj[:, js], float(P), tile_r[:, js], ALU.mult, ALU.add))
                nc.vector.tensor_copy(tile_eu[:, js], tile_e[:, js])
                nc.vector.tensor_copy(tile_ru[:, js], tile_r[:, js]).then_inc(table_ok, 1)
            dve.wait_ge(table_ok, 2)

            def tile_w1(j, i, first):
                e = dve.value_load(tile_eu[0:1, bass.ds(j, 1)], min_val=0, max_val=E - 1)
                if not first:
                    dve.wait_ge(f_h, j - 1)
                nc.vector.tensor_copy(w1t[i], w1_sb[:, bass.ds(e, 1), :, :].rearrange("p e c f -> p (e c) f"))\
                    .then_inc(f_w1, 1)

            def tile_meta(j, i, jj, first):
                dve.wait_ge(f_in[i], 16 * (jj + 1))
                if not first:
                    dve.wait_ge(f_out[i], 16 * jj)
                m, row = ymeta[i], xf[i]
                w_first, w_second, e_first, tok = (row[:, D + k:D + k + 1] for k in range(4))
                nc.vector.tensor_tensor(m[:, 0:1], tile_e[:, bass.ds(j, 1)], e_first, ALU.is_equal)
                nc.vector.tensor_scalar(m[:, 4:5], tok, float(TOK), float(i * P), ALU.is_ge, ALU.mult)
                link(nc.vector.tensor_tensor(m[:, 1:2], w_first, w_second, ALU.subtract))
                nc.vector.tensor_scalar(m[:, 3:4], m[:, 0:1], -float(RESULTS), float(RESULTS), ALU.mult, ALU.add)
                nc.vector.tensor_tensor(m[:, 5:6], m[:, 4:5], tok, ALU.add)
                link(nc.vector.scalar_tensor_tensor(m[:, 2:3], m[:, 1:2], m[:, 0:1], w_second, ALU.mult, ALU.add))
                link(nc.vector.tensor_tensor(ydest[i][:], m[:, 3:4], m[:, 5:6], ALU.add))

            def tiles(jj, base_, first, last):
                chain[:] = [0, base_]
                for i in range(TB):
                    j = TB * jj + i
                    if not last or i < TB - 2:
                        tile_w1(j + 2, i % 2, False)
                    if not last or i < TB - 1:
                        tile_meta(j + 1, (i + 1) % TB, jj + (i + 1) // TB, first and i < TB - 1)
                    dve.wait_ge(f_y, j + 1)
                    nc.vector.tensor_scalar(ys[i], banks[6 + i % 2][:, 0:D], ymeta[i][:, 2:3], None, ALU.mult).then_inc(f_ys, 1)

            dve.wait_ge(w1_in, 16 * E)
            tile_w1(0, 0, True)
            tile_w1(1, 1, True)
            tile_meta(0, 0, 0, True)
            links0 = chain[1] + chain[0]
            tiles(0, links0, True, False)
            with dve.Fori(1, TILES // TB - 1) as jj:
                tiles(jj, links0 + META_LINKS * TB * jj, False, False)
            tiles(TILES // TB - 1, links0 + META_LINKS * TB * (TILES // TB - 1), False, True)
            links1 = chain[1] + chain[0]

            def result(k, i, kk):
                dve.wait_ge(e_in[i], 32 * (kk + 1))
                y2 = xy[:, bass.ds(2 * k, 2), :].rearrange("p u d -> p (u d)")
                nc.vector.tensor_tensor(y2, y2, fin[i][:, 0, :], ALU.add).then_inc(dch, 1)
                dve.wait_ge(dch, links1 + k + 1)
                nc.vector.tensor_tensor(y2, y2, fin[i][:, 1, :], ALU.add).then_inc(e_add, 1)

            with dve.Fori(0, B // 2 // RB) as kk:
                for i in range(RB):
                    result(RB * kk + i, i, kk)

        @block.tensor
        def _(pe):
            def use(g, u):
                if not isinstance(g, int) or A_USES * g + u >= 2:
                    pe.wait_ge(a_free, A_USES * g + u - 1)
                return a_bank[u % 2]

            def stage_k(g):
                pe.wait_ge(ctx_in, 16 * (g + 1))
                for m in range(KC):
                    bank = use(g, m)
                    for c in range(KC):
                        last = nc.tensor.matmul(bank[:], wk_sb[:, c, m * P:(m + 1) * P], ctxg[:, c, :],
                                                start=c == 0, stop=c == KC - 1)
                    last.then_inc(a_done, 1)

            def stage_q(g):
                pe.wait_ge(xn_ok, g + 1)
                for c in range(KC):
                    bank = use(g, 2 + c)
                    for t in range(T):
                        last = nc.tensor.transpose(bank[:, t * P:(t + 1) * P], xn[:, t, c * P:(c + 1) * P], ident[:])
                    last.then_inc(a_done, 1)
                for m in range(KC):
                    bank = use(g, 4 + m)
                    for c in range(KC):
                        if m == 0:
                            pe.wait_ge(a_free, A_USES * g + 3 + c)
                        last = nc.tensor.matmul(bank[:], wq_sb[:, c, m * P:(m + 1) * P], xnT[:, c, :],
                                                start=c == 0, stop=c == KC - 1)
                    last.then_inc(a_done, 1)

            def hidden(g, c, u, pairs):
                pe.wait_ge(a_free, A_USES * g + 5 + c)
                for p in pairs:
                    bank = use(g, u + p)
                    nc.tensor.matmul(bank[:], g1_sb[:, p, :], qT[:, c, :], start=True, stop=True).then_inc(a_done, 1)

            def stage_gate(g, c, u, pairs=range(PAIRS)):
                hidden(g, c, u, pairs)
                gate(g, u)

            def gate(g, u):
                bank = use(g, u + PAIRS)
                for p in range(PAIRS):
                    pe.wait_ge(a_free, A_USES * g + u + p + 1)
                    last = nc.tensor.matmul(bank[2 * DH * p:2 * DH * (p + 1), :], g2_sb[:], hid[:, p, :],
                                            start=True, stop=True)
                last.then_inc(a_done, 1)

            def stage_v(g, ts=range(T)):
                for t in ts:
                    bank = use(g, 16 + t)
                    for c in range(KC):
                        last = nc.tensor.matmul(bank[:, 0:D], ctxg[:, c, t * P:(t + 1) * P], wv_sb[:, c, :],
                                                start=c == 0, stop=c == KC - 1)
                    last.then_inc(a_done, 1)

            def bias(bank, side):
                nc.tensor.matmul(bank[:], identb[:], bias_b[:, side, :].unsqueeze(1).to_broadcast([P, QH, P]),
                                 start=True, stop=False)

            def scores(n, g, par, t, c):
                if not isinstance(n, int) or NQ * n + c >= 2:
                    pe.wait_ge(max_done, NQ * n + c - 1)
                if t == 0 and c == 0:
                    pe.wait_ge(k_st, 16 * NT * (g + 1))
                if t == 0 and c % (NQ // KC) == 0:
                    pe.wait_ge(q_st[c // (NQ // KC)], 16 * NT * (g + 1))
                bank = sq_bank[c % 2]
                bias(bank, 0)
                for j in range(QH):
                    h = QH * c + j
                    last = nc.tensor.matmul(bank[:, j * P:(j + 1) * P], head(par, 0, h, t, KR),
                                            head(par, 1, h, t, KR), start=False, stop=j == QH - 1)
                last.then_inc(s_done, 1)

            def shifted(n, par, t, c):
                if not isinstance(n, int) or NQ * n + c >= 2:
                    pe.wait_ge(exp_done, NQ * n + c - 1)
                if c == 0:
                    pe.wait_ge(m_in, 16 * (n + 1))
                bank = sk_bank[c % 2]
                bias(bank, 1)
                for j in range(QH):
                    h = QH * c + j
                    last = nc.tensor.matmul(bank[:, j * P:(j + 1) * P], head(par, 1, h, t, KR + MR),
                                            head(par, 0, h, t, KR + MR), start=False, stop=j == QH - 1)
                last.then_inc(st_done, 1)

            def values(n, t, c, old1):
                pe.wait_ge(exp_done, NQ * n + c + 1)
                if c == 0 and old1:
                    pe.wait_ge(os_ok, n)
                for j in range(QH):
                    last = nc.tensor.matmul(o_bank[VW * j:VW * (j + 1), c * P:(c + 1) * P], v[:, t, QH * c + j, :],
                                            pT[:, c, j * P:(j + 1) * P], start=True, stop=True)
                last.then_inc(pv_done, 1)

            def max_rows(n):
                pe.wait_ge(m3_ok, n + 1)
                pe.sem_inc(pe_passed, 1)
                return nc.tensor.transpose(mT_ps, m3[:].rearrange("p s h -> p (s h)"), identb[:])

            pe.wait_ge(c_wk, 16)
            stage_k(0)
            pe.wait_ge(gelu_b, 1)
            for c in range(KC):
                last = nc.tensor.matmul(o_bank[:, c:c + 1], wb2_sb[:, c * P:(c + 1) * P], wb1g[:], start=True, stop=True)
            last.then_inc(base_mm, 1)
            pe.wait_ge(const_pool, CONST_IDENT)
            pe.wait_ge(c_wq, 16)
            stage_q(0)
            stage_gate(0, 0, 6)
            stage_gate(0, 1, 11)
            pe.wait_ge(c_wv, 16)
            stage_v(0)
            pe.wait_ge(const_dve, 4)
            pe.wait_ge(const_pool, CONST_MATRICES)
            for c in range(NQ):
                scores(0, 0, 0, 0, c)
            max_rows(0).then_inc(m_done, 1)
            scores(1, 0, 0, 1, 0)
            scores(1, 0, 0, 1, 1)
            pe.wait_ge(c_wo, 16)

            def bank_read(n, now):
                if now:
                    pe.wait_ge(mT_sb, n + 1)
                if not isinstance(n, int) or n >= 3:
                    pe.wait_ge(c_read, n - 2)

            def scores_of(g, par, t, ahead, c):
                over = (t + ahead) // T
                scores(T * g + t + ahead, g + over, par ^ over, (t + ahead) % T, c)

            def slot(g, par, t, a, now, nxt, nxt2, old1, old2):
                n = T * g + t
                for c in range(NQ):
                    if nxt and c < NQ - 2:
                        scores_of(g, par, t, 1, c + 2)
                    if now:
                        shifted(n, par, t, c)
                        if c:
                            values(n, t, c - 1, old1)
                    if c == 0 and old1:
                        pe.wait_ge(os_ok, n)
                        bank_read(n, now)
                        for k in range(NQ):
                            last = nc.tensor.transpose(u_bank[:, k * P:(k + 1) * P], oS[:, k, :], ident[:])
                        last.then_inc(nat_done, 1)
                    if c == 1 and (old1 or old2):
                        if old1:
                            pe.wait_ge(o_ok, n)
                        else:
                            bank_read(n, False)
                        if old2:
                            pe.wait_ge(x2_ok, n - 1)
                        for k in range(2 * KC):
                            of = (o, pay[t % 2])[k // KC]
                            if (old1, old2)[k // KC]:
                                last = nc.tensor.transpose(u_bank[:, k * P:(k + 1) * P], of[:, k % KC * P:(k % KC + 1) * P],
                                                           ident[:])
                        last.then_inc(turn_done, 1)
                if old1 or old2:
                    pe.wait_ge(turn_sb, n)
                    for k in range(KC):
                        if old1:
                            last = nc.tensor.matmul(u_bank[:, 0:D], turned[:, k, :], wo_sb[:, k, :],
                                                    start=k == 0, stop=k == KC - 1)
                    for k in range(KC):
                        if old2:
                            last = nc.tensor.matmul(u_bank[:, D:D + E], turned[:, KC + k, :], wr_sb[:, k, :],
                                                    start=k == 0, stop=k == KC - 1)
                    last.then_inc(lo_done, 1)
                if now:
                    values(n, t, NQ - 1, old1)
                if a and t == 0:
                    stage_k(g + 1)
                if a and t == 1:
                    hidden(g + 1, 1, 11, range(PAIRS // 2))
                if a and t == 3:
                    stage_v(g + 1, (2,))
                if a and t == 2:
                    stage_v(g + 1, (0,))
                if nxt2:
                    scores_of(g, par, t, 2, 0)
                if old1 or old2:
                    pe.wait_ge(lo_read, n)
                else:
                    pe.wait_ge(mT_sb, n + 1)
                if nxt:
                    max_rows(n + 1).then_inc(m_done, 1)
                if a and t == 0:
                    stage_q(g + 1)
                if a and t == 1:
                    hidden(g + 1, 1, 11, range(PAIRS // 2, PAIRS))
                if a and t == 2:
                    stage_v(g + 1, (1,))
                if a and t == 3:
                    stage_v(g + 1, (3,))
                if old2:
                    pe.wait_ge(hot_ok, n - 1)
                    if nxt:
                        pe.wait_ge(mT_sb, n + 2)
                    nc.tensor.matmul(u_bank[:, D:D + E], before[:], hotb[:], start=True, stop=True)
                    nc.tensor.matmul(u_bank[:, D + E:D + 2 * E], ones_b[:], hotb[:], start=True, stop=True)\
                        .then_inc(c_done, 1)
                if nxt2:
                    scores_of(g, par, t, 2, 1)
                if a and t == 0:
                    stage_gate(g + 1, 0, 6)
                if a and t == 1:
                    gate(g + 1, 11)

            for t in range(T):
                slot(0, 0, t, True, True, True, True, t >= 1, t >= 2)
            with pe.Fori(0, (G - 2) // 2) as gg:
                for par in (1, 0):
                    for t in range(T):
                        slot(2 * gg + 2 - par, par, t, True, True, True, True, True, True)
            for t in range(T):
                slot(G - 1, 1, t, False, True, t < T - 1, t < T - 2, True, True)
            slot(G, 0, 0, False, False, False, False, True, True)
            slot(G, 0, 1, False, False, False, False, False, True)

            pe.wait_ge(c_read, B)
            pe.wait_ge(w2_in, 16 * E * T)
            pe.wait_ge(table_ok, 2)

            def tile_x(j, i, k, jj):
                pe.wait_ge(f_in[k], 16 * (jj + 1))
                if not isinstance(j, int) or j >= 2:
                    pe.wait_ge(f_xts, j - 1)
                for c in range(KC):
                    last = nc.tensor.transpose(banks[i][:, c * P:(c + 1) * P], xf[k][:, c * P:(c + 1) * P], ident[:])
                last.then_inc(f_xt, 1)

            def tile_h(j, i):
                pe.wait_ge(f_xts, j + 1)
                pe.wait_ge(f_w1, j + 1)
                if not isinstance(j, int) or j >= 2:
                    pe.wait_ge(f_hs, j - 1)
                for f in range(FC):
                    for c in range(KC):
                        last = nc.tensor.matmul(banks[2 + i][:, f * P:(f + 1) * P], w1t[i][:, c, f * P:(f + 1) * P],
                                                xfT[i][:, c, :], start=c == 0, stop=c == KC - 1)
                last.then_inc(f_h, 1)

            def tile_y(j, i):
                e = pe.value_load(tile_eu[0:1, bass.ds(j, 1)], min_val=0, max_val=E - 1)
                pe.wait_ge(f_hs, j + 1)
                if not isinstance(j, int) or j >= 2:
                    pe.wait_ge(f_ys, j - 1)
                for f in range(FC):
                    last = nc.tensor.matmul(banks[6 + i][:, 0:D], hT[i][:, f * P:(f + 1) * P],
                                            w2_sb[:, bass.ds(e, 1), f, :].rearrange("p e f -> p (e f)"),
                                            start=f == 0, stop=f == FC - 1)
                last.then_inc(f_y, 1)

            def tiles(jj, last):
                for i in range(TB):
                    j = TB * jj + i
                    if not last or i < TB - 2:
                        tile_x(j + 2, i % 2, (i + 2) % TB, jj + (i + 2) // TB)
                    if not last or i < TB - 1:
                        tile_h(j + 1, (i + 1) % 2)
                    tile_y(j, i % 2)

            tile_x(0, 0, 0, 0)
            tile_x(1, 1, 1, 0)
            tile_h(0, 0)
            tiles(0, False)
            with pe.Fori(1, TILES // TB - 1) as jj:
                tiles(jj, False)
            tiles(TILES // TB - 1, True)


_INS = ["x", "ctxT", "mask", "maskT", "gx", "gf", "wqT", "wkT", "wvT", "woT", "wb1", "wb2T", "gate1", "gate2",
        "wr", "w1", "w2"]


def kernel(x, ctx_1024, mask_1x1xSxS2_bf1, g_xattn, g_ffn, L0_xattn_wq, L0_xattn_wk, L0_xattn_wv, L0_xattn_wo,
           L0_xattn_wb1, L0_xattn_wb2, L0_xattn_wg1, L0_xattn_wg2, L0_ffn_router_w, L0_ffn_w1, L0_ffn_w2):
    import numpy as np
    import concourse.bacc as bacc
    from concourse.bass_utils import run_bass_kernel_spmd

    mask = np.asarray(mask_1x1xSxS2_bf1)[0, 0].view(np.uint8)
    wg1, wg2 = np.asarray(L0_xattn_wg1), np.asarray(L0_xattn_wg2)
    gate1 = np.zeros((P, PAIRS, P), np.float32)
    gate2 = np.zeros((P, 2 * DH), np.float32)
    for a in range(2):
        for pair in range(PAIRS):
            row = 2 * DH * pair + DH * a
            gate1[row:row + DH, pair, HID * a:HID * (a + 1)] = wg1.T
        gate2[HID * a:HID * (a + 1), DH * a:DH * (a + 1)] = wg2.T
    arrays = {
        "x": np.asarray(x),
        "ctxT": np.asarray(ctx_1024).reshape(TOK, D).T,
        "mask": mask,
        "maskT": mask.T,
        "gx": np.asarray(g_xattn).reshape(1, 1),
        "gf": np.asarray(g_ffn).reshape(1, 1),
        "wqT": np.asarray(L0_xattn_wq).T,
        "wkT": np.asarray(L0_xattn_wk).T,
        "wvT": np.asarray(L0_xattn_wv).T,
        "woT": np.asarray(L0_xattn_wo).T,
        "wb1": np.asarray(L0_xattn_wb1),
        "wb2T": np.asarray(L0_xattn_wb2).T,
        "gate1": gate1,
        "gate2": gate2,
        "wr": np.asarray(L0_ffn_router_w),
        "w1": np.asarray(L0_ffn_w1),
        "w2": np.asarray(L0_ffn_w2),
    }
    nc = bacc.Bacc("TRN2", target_bir_lowering=False, num_devices=1)
    args = []
    for name in _INS:
        arrays[name] = np.ascontiguousarray(arrays[name])
        a = arrays[name]
        args.append(nc.dram_tensor(f"in_{name}", a.shape, mybir.dt.from_np(a.dtype), kind="ExternalInput").ap())
    args.append(nc.dram_tensor("out_0", (B, S, D), F32, kind="ExternalOutput").ap())
    build(nc, *args)
    got = run_bass_kernel_spmd(nc, [{f"in_{n}": arrays[n] for n in _INS}], core_ids=[0])
    return got.results[0]["out_0"]
```
